# Optimizing a Trainium2 kernel written in Bass

```python
import numpy as np
import jax
import jax.numpy as jnp

def _softmax(x, axis=-1):
    return jax.nn.softmax(x, axis=axis)

def _gelu(x):
    return jax.nn.gelu(x, approximate=True)

def _silu(x):
    return jax.nn.silu(x)

def _sigmoid(x):
    return jax.nn.sigmoid(x)

def _layernorm(x, axis=-1, eps=1e-05):
    m = jnp.mean(x, axis=axis, keepdims=True)
    v = jnp.var(x, axis=axis, keepdims=True)
    return (x - m) / jnp.sqrt(v + eps)

def _scatter_add(tgt, idx, src, axis=0):
    return tgt.at[idx].add(src)

def _segment_sum(src, seg, n):
    return jax.ops.segment_sum(src, seg, n)
kernel_name = 'mk_adaln_ffn_d1_seqx_r4_7bb747'

def setup_inputs(seed: int=0):
    np.random.seed(seed)
    _w = jnp.asarray

    def _rec_inputs():
        import jax
        import jax.numpy as jnp
        _rk = jax.random.key(seed)
        x = -0.0003929 + 0.9999 * jax.random.normal(jax.random.fold_in(_rk, 1), (32, 64, 1024), jnp.float32)
        _lenS = 64 - jax.random.randint(jax.random.fold_in(_rk, 7), (32,), 0, max(1, 64 // 4) + 1, jnp.int32)
        _lenS2 = 64 - jax.random.randint(jax.random.fold_in(_rk, 8), (32,), 0, max(1, 64 // 4) + 1, jnp.int32)
        itok_B_8_3872 = jax.random.randint(jax.random.fold_in(_rk, 11), (32,), 8, 3873, jnp.int32)
        return (x, itok_B_8_3872)
    x, itok_B_8_3872 = _rec_inputs()

    def _L0_cond_setup():
        import math
        import jax, jax.numpy as jnp
        import numpy as np
        H, N, B, L = (64, 64, 16, 1024)
        DT_MIN, DT_MAX = (0.001, 0.1)

        def _get_kernel(log_dt, C, log_A_real, A_imag, length):
            Cc = C[..., 0] + 1j * C[..., 1]
            dt = jnp.exp(log_dt)
            A = -jnp.exp(log_A_real) + 1j * A_imag
            dtA = A * dt[:, None]
            P = dtA[:, :, None] * jnp.arange(length, dtype=jnp.float32)
            Cs = Cc * (jnp.exp(dtA) - 1.0) / A
            K = 2.0 * jnp.einsum('hn,hnl->hl', Cs, jnp.exp(P)).real
            return K
        key = jax.random.key(seed)
        ks = jax.random.split(key, 6)
        u = jax.random.normal(ks[0], (B, H, L), dtype=jnp.float32)
        length = jax.random.randint(ks[1], (B,), 0, L)
        log_dt = jax.random.uniform(ks[2], (H,), dtype=jnp.float32) * (math.log(DT_MAX) - math.log(DT_MIN)) + math.log(DT_MIN)
        C = jax.random.normal(ks[3], (H, N, 2), dtype=jnp.float32)
        log_A_real = jnp.log(0.5 * jnp.ones((H, N), dtype=jnp.float32))
        A_imag = math.pi * jnp.broadcast_to(jnp.arange(N, dtype=jnp.float32), (H, N))
        D = jax.random.normal(ks[4], (H,), dtype=jnp.float32)
        return {'u': u, 'length': length, 'log_dt': log_dt, 'C': C, 'log_A_real': log_A_real, 'A_imag': A_imag, 'D': D}
    _L0_cond_all = _L0_cond_setup()
    _L0_cond_in = {k: v for k, v in _L0_cond_all.items() if k in ('log_dt', 'C', 'log_A_real', 'A_imag', 'D')}
    del _L0_cond_all

    def _L0_ffn_setup():
        import jax, jax.numpy as jnp
        import numpy as np
        NUM_EXPERTS = 16
        TOP_K = 2
        INTER = 112
        key = jax.random.key(seed)
        k1, k2, k3, k4, k5 = jax.random.split(key, 5)
        B, S, H = (4, 512, 1024)
        scale = 0.02
        return {'hid': jax.random.normal(k1, (B, S, H), dtype=jnp.float32), 'gate_w': jax.random.normal(k2, (NUM_EXPERTS, H), dtype=jnp.float32) * scale, 'u': jax.random.normal(k3, (NUM_EXPERTS * INTER, H), dtype=jnp.float32) * scale, 'g': jax.random.normal(k4, (NUM_EXPERTS * INTER, H), dtype=jnp.float32) * scale, 'd': jax.random.normal(k5, (H, NUM_EXPERTS * INTER), dtype=jnp.float32) * scale}
    _L0_ffn_all = _L0_ffn_setup()
    _L0_ffn_in = {k: v for k, v in _L0_ffn_all.items() if k in ('gate_w', 'u', 'g', 'd')}
    del _L0_ffn_all
    return {'x': x, 'itok_B_8_3872': itok_B_8_3872, 'L0_cond_log_dt': _L0_cond_in['log_dt'], 'L0_cond_C': _L0_cond_in['C'], 'L0_cond_log_A_real': _L0_cond_in['log_A_real'], 'L0_cond_A_imag': _L0_cond_in['A_imag'], 'L0_cond_D': _L0_cond_in['D'], 'L0_ffn_gate_w': _L0_ffn_in['gate_w'], 'L0_ffn_u': _L0_ffn_in['u'], 'L0_ffn_g': _L0_ffn_in['g'], 'L0_ffn_d': _L0_ffn_in['d']}

def reference(x, itok_B_8_3872, L0_cond_log_dt, L0_cond_C, L0_cond_log_A_real, L0_cond_A_imag, L0_cond_D, L0_ffn_gate_w, L0_ffn_u, L0_ffn_g, L0_ffn_d):
    import jax
    import jax.numpy as jnp

    def _L0_cond_ref(u, length, log_dt, C, log_A_real, A_imag, D):
        import math
        import jax, jax.numpy as jnp
        import numpy as np
        H, N, B, L = (64, 64, 16, 1024)
        DT_MIN, DT_MAX = (0.001, 0.1)

        def _get_kernel(log_dt, C, log_A_real, A_imag, length):
            Cc = C[..., 0] + 1j * C[..., 1]
            dt = jnp.exp(log_dt)
            A = -jnp.exp(log_A_real) + 1j * A_imag
            dtA = A * dt[:, None]
            P = dtA[:, :, None] * jnp.arange(length, dtype=jnp.float32)
            Cs = Cc * (jnp.exp(dtA) - 1.0) / A
            K = 2.0 * jnp.einsum('hn,hnl->hl', Cs, jnp.exp(P)).real
            return K
        Bq, Hq, Lq = u.shape
        mask = (jnp.arange(Lq) < length[:, None]).astype(u.dtype)
        u_m = u * mask[:, None, :]
        kernel = _get_kernel(log_dt, C, log_A_real, A_imag, Lq)
        n = 2 * Lq
        k_f = jnp.fft.rfft(kernel, n=n)
        u_f = jnp.fft.rfft(u_m, n=n)
        y = jnp.fft.irfft(u_f * k_f, n=n)[..., :Lq]
        y = y + u_m * D[:, None]
        return y * mask[:, None, :]

    def _L0_ffn_ref(hid, gate_w, u, g, d):
        import jax, jax.numpy as jnp
        import numpy as np
        NUM_EXPERTS = 16
        TOP_K = 2
        INTER = 112
        B, S, H = hid.shape
        x = hid.reshape(-1, H)
        bs = x.shape[0]
        logits = x @ gate_w.T
        probs = jax.nn.softmax(logits.astype(jnp.float32), axis=-1)
        vals, idx = jax.lax.top_k(probs, TOP_K)
        vals = vals / jnp.sum(vals, axis=-1, keepdims=True)
        rows = jnp.arange(bs)[:, None]
        w = jnp.zeros((bs, NUM_EXPERTS), dtype=jnp.float32).at[rows, idx].set(vals)
        w = w.astype(x.dtype)
        gate_out = (x @ g.T).reshape(bs, NUM_EXPERTS, INTER)
        up_out = (x @ u.T).reshape(bs, NUM_EXPERTS, INTER)
        h = jax.nn.silu(gate_out) * up_out
        d_r = d.reshape(H, NUM_EXPERTS, INTER)
        out = jnp.einsum('bei,hei,be->bh', h, d_r, w)
        return out.reshape(B, S, H)
    x = x + _L0_ffn_ref(_L0_cond_ref(x, itok_B_8_3872, L0_cond_log_dt, L0_cond_C, L0_cond_log_A_real, L0_cond_A_imag, L0_cond_D), L0_ffn_gate_w, L0_ffn_u, L0_ffn_g, L0_ffn_d)
    return x

_drawn_inputs = setup_inputs


def setup_inputs(seed=0):
    import zlib

    import numpy as np

    out = dict(_drawn_inputs(seed))
    spreads = {'L0_cond_log_A_real': (-0.6931471824645996, 0.2)}
    factors = {}
    for name, (base, spread) in spreads.items():
        noise = np.random.default_rng([zlib.crc32(name.encode()), seed]).standard_normal(out[name].shape)
        drawn = base * np.exp(spread * noise) if base else spread * noise
        out[name] = jnp.asarray(drawn.astype(out[name].dtype))
    for name, factor in factors.items():
        out[name] = (out[name] * factor).astype(out[name].dtype)
    return out
```

```python
import math
from contextlib import ExitStack

import concourse.bass as bass
from concourse import mybir

B, H, L = 32, 64, 1024
N = 64
P = 128
E, INTER, K = 16, 112, 2
TOK = B * H
C = L // P
HG = P // B
G = H // HG
LO = 32
SEG = 3 * LO
KROW = L + P
MT = -(-K * TOK // P) + E - 1

LOG2E = 1.0 / math.log(2.0)
LN2_HI = 0.693359375
LN2_LO = math.log(2.0) - LN2_HI
TWO_PI = 2.0 * math.pi
TWO_PI_HI = 6.28125
TWO_PI_MID = round((TWO_PI - TWO_PI_HI) * 2**20) / 2**20
TWO_PI_LO = TWO_PI - TWO_PI_HI - TWO_PI_MID
ROUND = 1.5 * 2.0**23
PI_IN = 3.1415925
EXP_TERMS = 9
GU = 2 * INTER
MC = MT + 1
WB = 4
OB = 3
NONE = 4 * K * TOK
HALF_DOWN = (P - 1) / (2.0 * P)


def build(nc, x_time, x_rows, lengths, log_dt, c_re, c_im, log_a, a_im, skip, gate_t, gu_t, d_t, out):
    fp32, i32, u32 = mybir.dt.float32, mybir.dt.int32, mybir.dt.uint32
    ALU, ACT, AX = mybir.AluOpType, mybir.ActivationFunctionType, mybir.AxisListType

    ctx = ExitStack()
    with ctx:
        def sb(name, shape, dt=fp32):
            return ctx.enter_context(nc.sbuf_tensor(name, shape, dt))

        def pb(name, shape, dt=fp32):
            return ctx.enter_context(nc.psum_tensor(name, shape, dt))

        def sem(name):
            return ctx.enter_context(nc.semaphore(name))

        k_rows = nc.dram_tensor("k_rows", [H, KROW], fp32)
        y_rows = nc.dram_tensor("y_rows", [TOK, L], fp32).ap()
        picks = nc.dram_tensor("picks", [K * TOK, L], fp32).ap()

        arena = sb("arena", [P, G, L])
        flat = arena[:, :, :].rearrange("p g l -> p (g l)")
        toep = flat[:, 0:2 * HG * L].rearrange("p (s h l) -> p s h l", s=2, h=HG)
        at = 2 * HG * L
        mag = flat[:, at:at + H * 2 * LO].rearrange("p (h l) -> p h l", h=H)
        at += H * 2 * LO
        u_t = flat[:, at:at + 2 * HG * C * B].rearrange("p (s h n) -> p s h n", s=2, h=HG)
        at += 2 * HG * C * B
        y_t = flat[:, at:at + 2 * C * P].rearrange("p (s c n) -> p s c n", s=2, c=C)
        slot_row = flat[:, 0:K * G * P].rearrange("p (j r) -> p j r", j=K * G)
        slot_tile = flat[:, K * G * P:K * G * (P + 2 * MC)].rearrange("p (j n) -> p j n", j=K * G)
        par = sb("par", [P, 5, H])
        LOGDT, LOGA, AIM, CRE, CIM = range(5)
        skip_row = sb("skip_row", [1, H])
        tmp = sb("tmp", [P, 24, H])
        tmp_i = sb("tmp_i", [P, 2, H], i32)
        decay = sb("decay", [P, H])
        omega = sb("omega", [P, H])
        cs_re = sb("cs_re", [P, H])
        cs_im = sb("cs_im", [P, H])
        steps = sb("steps", [P, SEG])
        off_turns = sb("off_turns", [P, SEG])
        off_rad = sb("off_rad", [P, SEG])
        phase = sb("phase", [P, 2, HG, SEG])
        turns = sb("turns", [P, 2, HG, SEG])
        angle = sb("angle", [P, 2, HG, SEG])
        wave = sb("wave", [P, 2, HG, SEG])
        am = sb("am", [P, 2, HG, LO])
        am2 = sb("am2", [P, 2, HG, LO])
        bm = sb("bm", [P, 2, HG, LO])
        k_sb = sb("k_sb", [LO, 2, HG, LO])
        zero = sb("zero", [H, P])
        y_tok = sb("y_tok", [P, 2, L])
        mask_t = sb("mask_t", [P, C, B])
        len_i = sb("len_i", [P, B], i32)
        len_f = sb("len_f", [P, B])
        time_col = sb("time_col", [P, C])
        ident = sb("ident", [P, P])
        gate_sb = sb("gate_sb", [P, C, E])
        logits = sb("logits", [P, G, E])
        top_v = sb("top_v", [P, G, 8])
        top_i = sb("top_i", [P, G, 8], u32)

        iota_row = sb("iota_row", [P, P])
        before = sb("before", [P, P])
        ones = sb("ones", [P, P])
        token_no = sb("token_no", [P, K * G])
        spread = sb("spread", [P, G, E])
        total = sb("total", [P, G])
        top2 = sb("top2", [P, K, G])
        weight = sb("weight", [P, K, G])
        norm = sb("norm", [P, G])
        expert = sb("expert", [P, K, G])
        chosen = sb("chosen", [P, K, G, E])
        both = sb("both", [P, G, E])
        count = sb("count", [P, G, E])
        run = sb("run", [P, 2, G, E])
        tiles = sb("tiles", [P, E])
        ends = sb("ends", [P, E])
        starts = sb("starts", [P, E])
        dest = sb("dest", [P, G, E])
        slot = sb("slot", [P, K * G])
        slot_q = sb("slot_q", [P, K * G])
        named = sb("named", [P, MC])
        shift = sb("shift", [P, MC])
        slot_weight = sb("slot_weight", [P, MC])
        from_row = sb("from_row", [P, MC], i32)
        to_row = sb("to_row", [P, MC], i32)
        passed = sb("passed", [P, MC, E])
        tile_e = sb("tile_e", [P, MC])
        tile_f = sb("tile_f", [P, 2, MC])
        tile_i = sb("tile_i", [P, 2, MC], i32)
        ends_i = sb("ends_i", [P, E], i32)

        w_gu = sb("w_gu", [P, WB * C * GU])
        w_d = sb("w_d", [INTER, WB * L])
        ys = sb("ys", [P, 2, L])
        ys_t = sb("ys_t", [P, 2, C, P])
        weight_now = sb("weight_now", [P, 2])
        silu = sb("silu", [P, 2, INTER])
        hid = sb("hid", [P, 2, INTER])
        hid_t = sb("hid_t", [INTER, 2, P])
        od = sb("od", [P, 2, L])
        pair = w_gu[:, 0:OB * K * L].rearrange("p (s k l) -> p s k l", s=OB, k=K)

        conv_ps = pb("conv_ps", [P, HG, 512])
        k_ps = pb("k_ps", [LO, HG, LO])
        before_ps = conv_ps[:, 0, 0:G * E].rearrange("p (g e) -> p g e", g=G)
        count_ps = conv_ps[:, 1, 0:G * E].rearrange("p (g e) -> p g e", g=G)
        table_ps = conv_ps[:, 2, 0:2 * MC]
        down_ps = conv_ps[:, 0:2, :]
        gu_ps = conv_ps[:, 2, 0:GU]
        hid_ps = conv_ps[0:INTER, 3, 0:P]
        log_ps = pb("log_ps", [P, E])
        ytr_ps = pb("ytr_ps", [P, L])

        par_in = sem("par_in")
        len_in = sem("len_in")
        gate_in = sem("gate_in")
        zero_made = sem("zero_made")
        pads_out = sem("pads_out")
        chain = sem("chain")
        act_chain = sem("act_chain")
        pool_chain = sem("pool_chain")
        half_sin = sem("half_sin")
        trig_in = sem("trig_in")
        decay_made = sem("decay_made")
        omega_made = sem("omega_made")
        coef_made = sem("coef_made")
        consts_made = sem("consts_made")
        mask_ready = sem("mask_ready")
        growth_made = sem("growth_made")
        mag_made = sem("mag_made")
        phase_made = sem("phase_made")
        angle_steps = sem("angle_steps")
        angle_made = sem("angle_made")
        wave_made = sem("wave_made")
        am_steps = sem("am_steps")
        factors_made = sem("factors_made")
        k_made = sem("k_made")
        k_copied = sem("k_copied")
        k_added = sem("k_added")
        k_stored = [sem(f"k_stored{i}") for i in range(2)]
        toep_in = [sem(f"toep_in{i}") for i in range(2)]
        u_in = [sem(f"u_in{i}") for i in range(2)]
        conv_done = sem("conv_done")
        conv_read = sem("conv_read")
        post_done = sem("post_done")
        ytr_read = sem("ytr_read")
        log_read = sem("log_read")
        top_made = sem("top_made")
        y_stored = [sem(f"y_stored{i}") for i in range(2)]

        top_found = sem("top_found")
        spread_made = sem("spread_made")
        spread_exp = sem("spread_exp")
        chosen_made = sem("chosen_made")
        counted = sem("counted")
        slots_made = sem("slots_made")
        table_made = sem("table_made")
        lists_made = sem("lists_made")
        experts_made = sem("experts_made")
        ends_made = sem("ends_made")
        weights_ready = sem("weights_ready")
        gu_done = sem("gu_done")
        yst_act = sem("yst_act")
        yst_dve = sem("yst_dve")
        silu_made = sem("silu_made")
        hid_made = sem("hid_made")
        turned = sem("turned")
        hid_turned = sem("hid_turned")
        hid_read = sem("hid_read")
        down_done = sem("down_done")
        od_act = sem("od_act")
        od_dve = sem("od_dve")
        weight_copied = sem("weight_copied")
        x_in = sem("x_in")
        pair_sum = sem("pair_sum")
        out_made = sem("out_made")
        w_in = [sem(f"w_in{i}") for i in range(WB)]
        gathered = [sem(f"gathered{i}") for i in range(2)]
        scattered = [sem(f"scattered{i}") for i in range(2)]
        pair_in = [sem(f"pair_in{i}") for i in range(OB)]
        out_stored = sem("out_stored")

        block = ctx.enter_context(nc.Block())

        def hs(g):
            return bass.ds(g * HG, HG)

        @block.sync
        def _(sp):
            for part in range(2):
                rows = slice(part * N, part * N + N)
                sp.dma_start(par[rows, LOGDT, :], log_dt.partition_broadcast(N)).then_inc(par_in, 16)
                sp.dma_start(par[rows, LOGA, :], log_a).then_inc(par_in, 16)
                sp.dma_start(par[rows, AIM, :], a_im).then_inc(par_in, 16)
                sp.dma_start(par[rows, CRE, :], c_re).then_inc(par_in, 16)
                sp.dma_start(par[rows, CIM, :], c_im).then_inc(par_in, 16)
            sp.dma_start(skip_row[:, :], skip).then_inc(par_in, 16)
            sp.dma_start(len_i[:, :], lengths.partition_broadcast(P)).then_inc(len_in, 16)
            sp.dma_start(gate_sb[:, :, :], gate_t).then_inc(gate_in, 16)
            sp.wait_ge(zero_made, 1)
            sp.dma_start(k_rows.ap()[:, 0:P - 1], zero[:, 0:P - 1]).then_inc(pads_out, 16)
            sp.wait_ge(pads_out, 16)

            def load_expert(e):
                s = e % WB
                sp.dma_start(w_gu[:, s * C * GU:(s + 1) * C * GU], gu_t[e]).then_inc(w_in[s], 16)
                sp.dma_start(w_d[:, s * L:(s + 1) * L], d_t[e]).then_inc(w_in[s], 16)

            for g in range(G):
                p, i = g % 2, g // 2
                sp.wait_ge(k_added, g + 1)
                sp.dma_start(bass.AP(k_rows, g * HG * KROW + P - 1, [[LO, LO], [KROW, HG], [1, LO]]),
                             k_sb[:, p, :, :]).then_inc(k_stored[p], 16)
                if g >= 2:
                    sp.wait_ge(conv_done, (g - 1) * HG)
                sp.dma_start(u_t[:, p, :, :], x_time[:, g * HG:(g + 1) * HG, :]).then_inc(u_in[p], 16)
                sp.wait_ge(k_stored[p], 16 * (i + 1))
                sp.dma_start(toep[:, p, :, :], bass.AP(k_rows, g * HG * KROW, [[1, P], [KROW, HG], [1, L]])
                             ).then_inc(toep_in[p], 16)
                if g >= G - WB:
                    load_expert(g - (G - WB))
            for e in range(WB):
                sp.wait_ge(w_in[e % WB], 32)
                sp.sem_inc(weights_ready, 1)
            sp.wait_ge(ends_made, 1)
            sp.wait_ge(lists_made, 1)
            for e in range(WB, E):
                end = sp.value_load(ends_i[0:1, e - WB:e - WB + 1], min_val=1, max_val=MT)
                sp.wait_ge(down_done, end)
                load_expert(e)
                sp.wait_ge(w_in[e % WB], 32 * (e // WB + 1))
                sp.sem_inc(weights_ready, 1)
                for g in range(e - WB, G, E - WB):
                    sp.dma_start(arena[:, g, :], x_rows[g * P:(g + 1) * P, :]).then_inc(x_in, 16)
            sp.wait_ge(scattered[0], 16 * ((MT + 1) // 2))
            sp.wait_ge(scattered[1], 16 * (MT // 2))
            for g in range(G):
                if g >= OB:
                    sp.wait_ge(pair_sum, g - OB + 1)
                sp.dma_start(pair[:, g % OB, :, :],
                             picks.rearrange("(k t) l -> t k l", k=K)[g * P:(g + 1) * P, :, :]
                             ).then_inc(pair_in[g % OB], 16)

        @block.gpsimd
        def _(pool):
            made = [0]

            def link(ins):
                made[0] += 1
                ins.then_inc(pool_chain, 1)
                pool.wait_ge(pool_chain, made[0])

            nc.gpsimd.memset(zero[:, :], 0.0).then_inc(zero_made, 1)
            for k, m in ((0, LO), (1, LO), (2, 1)):
                nc.gpsimd.iota(steps[:, k * LO:(k + 1) * LO], [[m, LO]], base=0, channel_multiplier=0,
                               allow_small_or_imprecise_dtypes=True)
            nc.gpsimd.iota(time_col[:, :], [[P, C]], base=0, channel_multiplier=1,
                           allow_small_or_imprecise_dtypes=True)
            nc.gpsimd.iota(iota_row[:, :], [[1, P]], base=0, channel_multiplier=0,
                           allow_small_or_imprecise_dtypes=True)
            nc.gpsimd.iota(token_no[:, :], [[P, K * G]], base=1, channel_multiplier=1,
                           allow_small_or_imprecise_dtypes=True)
            nc.gpsimd.memset(ys[:, :, :], 0.0)
            nc.gpsimd.memset(ones[:, :], 1.0)
            link(nc.gpsimd.memset(before[:, :], 1.0))
            nc.gpsimd.affine_select(out=before[:, :], in_=before[:, :], compare_op=ALU.is_gt, fill=0.0,
                                    base=0, pattern=[[1, P]], channel_multiplier=-1)
            link(nc.gpsimd.memset(ident[:, :], 0.0))
            nc.gpsimd.affine_select(out=ident[:, :], in_=ident[:, :], compare_op=ALU.not_equal, fill=1.0,
                                    base=0, pattern=[[-1, P]], channel_multiplier=1).then_inc(consts_made, 1)
            pool.wait_ge(consts_made, 1)
            pool.wait_ge(decay_made, 1)
            nc.gpsimd.tensor_tensor(mag[:, :, :], decay[:, :].unsqueeze(2).to_broadcast([P, H, 2 * LO]),
                                    steps[:, LO:].unsqueeze(1).to_broadcast([P, H, 2 * LO]),
                                    ALU.mult).then_inc(growth_made, 1)

            def phases(g, p, first):
                if not first:
                    pool.wait_ge(angle_made, g - 1)
                nc.gpsimd.tensor_tensor(phase[:, p, :, :],
                                        omega[:, hs(g)].unsqueeze(2).to_broadcast([P, HG, SEG]),
                                        steps[:, :].unsqueeze(1).to_broadcast([P, HG, SEG]),
                                        ALU.mult).then_inc(phase_made, 1)

            def factors(g, p, first):
                pool.wait_ge(wave_made, g + 1)
                if not first:
                    pool.wait_ge(k_made, g - 1)
                bc = [P, HG, LO]
                nc.gpsimd.tensor_tensor(am[:, p, :, :], wave[:, p, :, 0:LO],
                                        cs_re[:, hs(g)].unsqueeze(2).to_broadcast(bc), ALU.mult).then_inc(am_steps, 1)
                nc.gpsimd.tensor_tensor(am2[:, p, :, :], wave[:, p, :, LO:2 * LO],
                                        cs_im[:, hs(g)].unsqueeze(2).to_broadcast(bc), ALU.mult).then_inc(am_steps, 1)
                nc.gpsimd.tensor_tensor(bm[:, p, :, :], wave[:, p, :, 2 * LO:], mag[:, hs(g), LO:],
                                        ALU.mult).then_inc(am_steps, 1)
                pool.wait_ge(am_steps, 4 * g + 3)
                nc.gpsimd.tensor_tensor(am[:, p, :, :], am[:, p, :, :], am2[:, p, :, :], ALU.add).then_inc(am_steps, 1)
                pool.wait_ge(am_steps, 4 * g + 4)
                nc.gpsimd.tensor_tensor(am[:, p, :, :], am[:, p, :, :], mag[:, hs(g), 0:LO],
                                        ALU.mult).then_inc(factors_made, 1)

            pool.wait_ge(omega_made, 1)
            for p in range(2):
                phases(p, p, True)
            pool.wait_ge(coef_made, 1)
            pool.wait_ge(mag_made, 1)
            for p in range(2):
                factors(p, p, True)
                phases(2 + p, p, False)
            with pool.Fori(1, G // 2 - 1) as i:
                for p in range(2):
                    factors(2 * i + p, p, False)
                    phases(2 * i + 2 + p, p, False)
            for p in range(2):
                factors(G - 2 + p, p, False)

            def gather(t):
                if t >= 2:
                    pool.wait_ge(turned, t - 1)
                nc.gpsimd.indirect_dma_start(
                    out=ys[:, t % 2, :], out_offset=None, in_=y_rows,
                    in_offset=bass.IndirectOffsetOnAxis(ap=from_row[:, t:t + 1], axis=0),
                    bounds_check=TOK - 1, oob_is_err=False).then_inc(gathered[t % 2], 16)

            def scatter(t):
                pool.wait_ge(od_act, t + 1)
                pool.wait_ge(od_dve, t + 1)
                nc.gpsimd.indirect_dma_start(
                    out=picks, out_offset=bass.IndirectOffsetOnAxis(ap=to_row[:, t:t + 1], axis=0),
                    in_=od[:, t % 2, :], in_offset=None,
                    bounds_check=K * TOK - 1, oob_is_err=False).then_inc(scattered[t % 2], 16)

            pool.wait_ge(lists_made, 1)
            for p in range(2):
                pool.wait_ge(y_stored[p], 16 * (G // 2))
            gather(0)
            gather(1)
            for t in range(MT + 2):
                if t + 2 < MT:
                    gather(t + 2)
                if t >= 2:
                    scatter(t - 2)

        @block.scalar
        def _(act):
            act.wait_ge(growth_made, 1)
            nc.scalar.activation(mag[:, :, :], mag[:, :, :], ACT.Exp).then_inc(mag_made, 1)
            act.wait_ge(trig_in, 1)
            nc.scalar.activation(tmp[:, 10, :], tmp[:, 9, :], ACT.Sin, scale=0.5)
            nc.scalar.activation(tmp[:, 11, :], tmp[:, 9, :], ACT.Sin).then_inc(half_sin, 1)

            def waves(g, p, first):
                act.wait_ge(angle_made, g + 1)
                if not first:
                    act.wait_ge(factors_made, g - 1)
                nc.scalar.activation(wave[:, p, :, :], angle[:, p, :, :], ACT.Sin).then_inc(wave_made, 1)

            def rows_out(g, p, i, first):
                act.wait_ge(post_done, g + 1)
                if not first:
                    act.wait_ge(y_stored[p], 16 * i)
                nc.scalar.copy(y_tok[:, p, :], ytr_ps[:, :]).then_inc(ytr_read, 1)
                act.wait_ge(ytr_read, g + 1)
                act.dma_start(y_rows[bass.ds(g * P, P), :], y_tok[:, p, :]).then_inc(y_stored[p], 16)

            for g in range(5):
                waves(g, g % 2, g < 2)
            for p in range(2):
                rows_out(p, p, 0, True)
                waves(5 + p, 1 - p, False)
            with act.Fori(1, (G - 6) // 2) as i:
                for p in range(2):
                    rows_out(2 * i + p, p, i, False)
                    waves(2 * i + 5 + p, 1 - p, False)
            for g in range(G - 6, G):
                rows_out(g, g % 2, g // 2, False)
                if g + 5 < G:
                    waves(g + 5, (g + 5) % 2, False)

            act.wait_ge(spread_made, 1)
            nc.scalar.activation(spread[:, :, :], spread[:, :, :], ACT.Exp)
            nc.scalar.activation(top2[:, :, :], top2[:, :, :], ACT.Exp).then_inc(spread_exp, 1)

            def turn_half(t, p, first):
                act.wait_ge(turned, t + 1)
                if not first:
                    act.wait_ge(gu_done, t - 1)
                nc.scalar.copy(ys_t[:, p, 0:C // 2, :], ytr_ps[:, 0:L // 2].rearrange("p (c n) -> p c n", n=P)
                               ).then_inc(yst_act, 1)

            def gate(t, p, first):
                act.wait_ge(gu_done, t + 1)
                if not first:
                    act.wait_ge(hid_made, t - 1)
                nc.scalar.activation(silu[:, p, :], gu_ps[:, 0:INTER], ACT.Silu).then_inc(silu_made, 1)

            def weigh_half(t, p, i, first):
                act.wait_ge(down_done, t + 1)
                act.wait_ge(weight_copied, t + 1)
                if not first:
                    act.wait_ge(scattered[p], 16 * i)
                nc.scalar.mul(od[:, p, 0:L // 2], down_ps[:, 0, :], weight_now[:, p:p + 1]).then_inc(od_act, 1)

            turn_half(0, 0, True)
            gate(0, 0, True)
            turn_half(1, 1, True)
            gate(1, 1, True)
            turn_half(2, 0, False)
            weigh_half(0, 0, 0, True)
            gate(2, 0, False)
            turn_half(3, 1, False)
            weigh_half(1, 1, 0, True)
            with act.Fori(1, (MT - 3) // 2) as i:
                for p in (1, 0):
                    gate(2 * i + 2 - p, p, False)
                    turn_half(2 * i + 3 - p, 1 - p, False)
                    weigh_half(2 * i + 1 - p, 1 - p, i, False)
            for t in range(MT - 2, MT):
                gate(t, t % 2, False)
                if t + 1 < MT:
                    turn_half(t + 1, (t + 1) % 2, False)
                weigh_half(t - 1, (t - 1) % 2, (t - 1) // 2, False)
            weigh_half(MT - 1, (MT - 1) % 2, (MT - 1) // 2, False)
            for g in range(G):
                act.wait_ge(out_made, g + 1)
                act.dma_start(out[g * P:(g + 1) * P, :], arena[:, g, :]).then_inc(out_stored, 16)
            act.wait_ge(out_stored, 16 * G)

        @block.vector
        def _(dve):
            made = [0]

            def link(ins):
                made[0] += 1
                ins.then_inc(chain, 1)
                dve.wait_ge(chain, made[0])

            def tt(out, a, b, op):
                link(nc.vector.tensor_tensor(out, a, b, op))

            def ts(out, a, s1, s2, op0, op1):
                link(nc.vector.tensor_scalar(out, a, s1, s2, op0, op1))

            def stt(out, a, s, b, op0, op1):
                link(nc.vector.scalar_tensor_tensor(out, a, s, b, op0, op1))

            def t(i, n=1):
                return tmp[:, i, :] if n == 1 else tmp[:, i:i + n, :]

            for part, quarters in ((0, (1, 2, 1)), (1, (2, -1, 0))):
                for k, q in enumerate(quarters):
                    rows, cols = slice(part * N, part * N + N), slice(k * LO, (k + 1) * LO)
                    link(nc.vector.memset(off_turns[rows, cols], q * 0.25))
                    link(nc.vector.memset(off_rad[rows, cols], q * 0.25 * TWO_PI))
            dve.wait_ge(par_in, 16 * 11)
            logs = par[:, LOGDT:LOGA + 1, :]
            k2, r2, p2 = t(0, 2), t(2, 2), t(4, 2)
            ts(k2, logs, LOG2E, ROUND, ALU.mult, ALU.add)
            ts(k2, k2, ROUND, -126.0, ALU.subtract, ALU.max)
            stt(r2, k2, -LN2_HI, logs, ALU.mult, ALU.add)
            stt(r2, k2, -LN2_LO, r2, ALU.mult, ALU.add)
            ts(p2, r2, 1.0 / math.factorial(EXP_TERMS), None, ALU.mult, ALU.bypass)
            for n in range(EXP_TERMS - 1, 0, -1):
                stt(p2, p2, 1.0 / math.factorial(n), r2, ALU.add, ALU.mult)
            ts(tmp_i[:, :, :], k2, 127.0, 2.0**23, ALU.add, ALU.mult)
            stt(p2, p2, 1.0, tmp_i[:, :, :].bitcast(fp32), ALU.add, ALU.mult)
            dt, a_abs, a_imag = t(4), t(5), par[:, AIM, :]
            link(nc.vector.scalar_tensor_tensor(decay[:, :], a_abs, -1.0, dt, ALU.mult, ALU.mult))
            nc.vector.tensor_tensor(omega[:, :], a_imag, dt, ALU.mult).then_inc(omega_made, 1)
            dve.wait_ge(omega_made, 1)
            dve.sem_inc(decay_made, 1)
            ts(t(8), omega[:, :], 1.0 / TWO_PI, ROUND, ALU.mult, ALU.add)
            ts(t(8), t(8), ROUND, None, ALU.subtract, ALU.bypass)
            stt(t(9), t(8), -TWO_PI_HI, omega[:, :], ALU.mult, ALU.add)
            stt(t(9), t(8), -TWO_PI_MID, t(9), ALU.mult, ALU.add)
            stt(t(9), t(8), -TWO_PI_LO, t(9), ALU.mult, ALU.add)
            nc.vector.tensor_scalar(t(9), t(9), PI_IN, -PI_IN, ALU.min, ALU.max).then_inc(trig_in, 1)
            ts(t(12), decay[:, :], 1.0 / 16.0, None, ALU.mult, ALU.bypass)
            ts(t(13), t(12), 1.0 / math.factorial(EXP_TERMS), None, ALU.mult, ALU.bypass)
            for n in range(EXP_TERMS - 1, 0, -1):
                stt(t(13), t(13), 1.0 / math.factorial(n), t(12), ALU.add, ALU.mult)
            for n in range(4):
                stt(t(13), t(13), 2.0, t(13), ALU.add, ALU.mult)
            dve.wait_ge(half_sin, 1)
            stt(t(14), t(10), 2.0, t(10), ALU.mult, ALU.mult)
            ts(t(15), t(14), -1.0, 1.0, ALU.mult, ALU.add)
            tt(t(15), t(15), t(13), ALU.mult)
            tt(t(15), t(15), t(14), ALU.subtract)
            stt(t(16), t(13), 1.0, t(11), ALU.add, ALU.mult)
            cre, cim = par[:, CRE, :], par[:, CIM, :]
            tt(t(17), cre, t(15), ALU.mult)
            tt(t(18), cim, t(16), ALU.mult)
            tt(t(17), t(17), t(18), ALU.subtract)
            tt(t(18), cre, t(16), ALU.mult)
            tt(t(19), cim, t(15), ALU.mult)
            tt(t(18), t(18), t(19), ALU.add)
            tt(t(19), a_abs, a_abs, ALU.mult)
            tt(t(20), a_imag, a_imag, ALU.mult)
            tt(t(19), t(19), t(20), ALU.add)
            link(nc.vector.reciprocal(t(19), t(19)))
            tt(t(20), t(18), a_imag, ALU.mult)
            tt(t(21), t(17), a_abs, ALU.mult)
            tt(t(20), t(20), t(21), ALU.subtract)
            stt(cs_re[:, :], t(20), 2.0, t(19), ALU.mult, ALU.mult)
            tt(t(20), t(18), a_abs, ALU.mult)
            tt(t(21), t(17), a_imag, ALU.mult)
            tt(t(20), t(20), t(21), ALU.add)
            nc.vector.scalar_tensor_tensor(cs_im[:, :], t(20), -2.0, t(19), ALU.mult, ALU.mult).then_inc(coef_made, 1)

            def angles(g, p, first):
                dve.wait_ge(phase_made, g + 1)
                off_t = off_turns[:, :].unsqueeze(1).to_broadcast([P, HG, SEG])
                off_r = off_rad[:, :].unsqueeze(1).to_broadcast([P, HG, SEG])
                ph, tu, an = phase[:, p, :, :], turns[:, p, :, :], angle[:, p, :, :]
                nc.vector.scalar_tensor_tensor(tu, ph, 1.0 / TWO_PI, off_t, ALU.mult, ALU.add).then_inc(angle_steps, 1)
                dve.wait_ge(angle_steps, 6 * g + 1)
                nc.vector.tensor_scalar(tu, tu, ROUND, ROUND, ALU.add, ALU.subtract).then_inc(angle_steps, 1)
                dve.wait_ge(angle_steps, 6 * g + 2)
                if not first:
                    dve.wait_ge(wave_made, g - 1)
                nc.vector.scalar_tensor_tensor(an, tu, -TWO_PI_HI, ph, ALU.mult, ALU.add).then_inc(angle_steps, 1)
                dve.wait_ge(angle_steps, 6 * g + 3)
                nc.vector.scalar_tensor_tensor(an, tu, -TWO_PI_MID, an, ALU.mult, ALU.add).then_inc(angle_steps, 1)
                dve.wait_ge(angle_steps, 6 * g + 4)
                nc.vector.scalar_tensor_tensor(an, tu, -TWO_PI_LO, an, ALU.mult, ALU.add).then_inc(angle_steps, 1)
                dve.wait_ge(angle_steps, 6 * g + 5)
                nc.vector.tensor_tensor(an, an, off_r, ALU.add).then_inc(angle_steps, 1)
                dve.wait_ge(angle_steps, 6 * g + 6)
                nc.vector.tensor_scalar(an, an, PI_IN, -PI_IN, ALU.min, ALU.max).then_inc(angle_made, 1)

            def kernel_rows(g, p, i, first):
                dve.wait_ge(k_made, g + 1)
                if not first:
                    dve.wait_ge(k_stored[p], 16 * i)
                nc.vector.tensor_copy(k_sb[:, p, :, :], k_ps[:, :, :]).then_inc(k_copied, 1)
                dve.wait_ge(k_copied, g + 1)
                nc.vector.tensor_tensor(k_sb[0:1, p, :, 0], k_sb[0:1, p, :, 0], skip_row[0:1, hs(g)],
                                        ALU.add).then_inc(k_added, 1)

            def outputs(g, p, first):
                if not first:
                    dve.wait_ge(post_done, g - 1)
                for h in range(HG):
                    dve.wait_ge(conv_done, g * HG + h + 1)
                    nc.vector.tensor_tensor(y_t[:, p, :, h * B:(h + 1) * B],
                                            conv_ps[:, h, 0:C * B].rearrange("p (c b) -> p c b", c=C),
                                            mask_t[:, :, :], ALU.mult).then_inc(conv_read, 1)

            def router(g):
                dve.wait_ge(post_done, g + 1)
                nc.vector.tensor_copy(logits[:, bass.ds(g, 1), :], log_ps[:, :].unsqueeze(1)).then_inc(log_read, 1)

            dve.wait_ge(len_in, 16)
            dve.wait_ge(consts_made, 1)
            link(nc.vector.tensor_copy(len_f[:, :], len_i[:, :]))
            for c in range(C):
                last = nc.vector.tensor_scalar(mask_t[:, c, :], len_f[:, :], time_col[:, c:c + 1], None,
                                               ALU.is_gt, ALU.bypass)
            last.then_inc(mask_ready, 1)
            angles(0, 0, True)
            angles(1, 1, True)
            kernel_rows(0, 0, 0, True)
            angles(2, 0, False)
            kernel_rows(1, 1, 0, True)
            angles(3, 1, False)
            dve.wait_ge(mask_ready, 1)
            kernel_rows(2, 0, 1, False)
            outputs(0, 0, True)
            angles(4, 0, False)
            kernel_rows(3, 1, 1, False)
            outputs(1, 1, True)
            router(0)
            angles(5, 1, False)
            with dve.Fori(1, (G - 4) // 2) as i:
                for p in range(2):
                    kernel_rows(2 * i + 2 + p, p, i + 1, False)
                    outputs(2 * i + p, p, False)
                    router(2 * i + p - 1)
                    angles(2 * i + 4 + p, p, False)
            for g in range(G - 4, G):
                if g + 2 < G:
                    kernel_rows(g + 2, g % 2, (g + 2) // 2, False)
                outputs(g, g % 2, False)
                router(g - 1)
            router(G - 1)

            dve.wait_ge(log_read, G)
            for g in range(G):
                nc.vector.max(top_v[:, g, :], logits[:, g, :]).then_inc(top_found, 1)
            dve.wait_ge(top_found, G)
            tt(spread[:, :, :], logits[:, :, :], top_v[:, :, 0:1].to_broadcast([P, G, E]), ALU.subtract)
            nc.vector.tensor_tensor(top2[:, :, :], top_v[:, :, 0:K].rearrange("p g k -> p k g"),
                                    top_v[:, :, 0].unsqueeze(1).to_broadcast([P, K, G]),
                                    ALU.subtract).then_inc(spread_made, 1)
            for g in range(G):
                nc.vector.max_index(top_i[:, g, :], top_v[:, g, :], logits[:, g, :]).then_inc(top_made, 1)
            dve.wait_ge(top_made, G)
            link(nc.vector.tensor_copy(expert[:, :, :], top_i[:, :, 0:K].rearrange("p g k -> p k g")))
            tt(chosen[:, :, :, :].rearrange("p k g e -> p (k g) e"),
               expert[:, :, :].rearrange("p k g -> p (k g)").unsqueeze(2).to_broadcast([P, K * G, E]),
               iota_row[:, 0:E].unsqueeze(1).to_broadcast([P, K * G, E]), ALU.is_equal)
            nc.vector.tensor_tensor(both[:, :, :], chosen[:, 0, :, :], chosen[:, 1, :, :],
                                    ALU.add).then_inc(chosen_made, 1)
            dve.wait_ge(spread_exp, 1)
            link(nc.vector.reduce_sum(total[:, :], spread[:, :, :], AX.X))
            link(nc.vector.reciprocal(total[:, :], total[:, :]))
            tt(weight[:, :, :], top2[:, :, :], total[:, :].unsqueeze(1).to_broadcast([P, K, G]), ALU.mult)
            tt(norm[:, :], weight[:, 0, :], weight[:, 1, :], ALU.add)
            link(nc.vector.reciprocal(norm[:, :], norm[:, :]))
            tt(weight[:, :, :], weight[:, :, :], norm[:, :].unsqueeze(1).to_broadcast([P, K, G]), ALU.mult)
            dve.wait_ge(counted, 1)
            link(nc.vector.tensor_copy(count[:, :, :], count_ps))
            now, s, n = count[:, :, :], 1, 0
            while s < G:
                nxt = run[:, n % 2, :, :]
                link(nc.vector.tensor_copy(nxt[:, 0:s, :], now[:, 0:s, :]))
                tt(nxt[:, s:, :], now[:, s:, :], now[:, 0:G - s, :], ALU.add)
                now, s, n = nxt, 2 * s, n + 1
            ts(tiles[:, :], now[:, G - 1, :], 1.0 / P, HALF_DOWN, ALU.mult, ALU.add)
            ts(tiles[:, :], tiles[:, :], ROUND, ROUND, ALU.add, ALU.subtract)
            ts(tiles[:, :], tiles[:, :], 1.0, None, ALU.max, ALU.bypass)
            link(nc.vector.tensor_tensor_scan(ends[:, :], ones[:, 0:E], tiles[:, :], 0.0, ALU.mult, ALU.add))
            nc.vector.tensor_copy(ends_i[:, :], ends[:, :]).then_inc(ends_made, 1)
            tt(starts[:, :], ends[:, :], tiles[:, :], ALU.subtract)
            tt(dest[:, :, :], now, count[:, :, :], ALU.subtract)
            tt(dest[:, :, :], dest[:, :, :], before_ps, ALU.add)
            link(nc.vector.scalar_tensor_tensor(dest[:, :, :], starts[:, :].unsqueeze(1).to_broadcast([P, G, E]),
                                                float(P), dest[:, :, :], ALU.mult, ALU.add))
            for k in range(K):
                tt(chosen[:, k, :, :], chosen[:, k, :, :], dest[:, :, :], ALU.mult)
            link(nc.vector.reduce_sum(slot[:, :], chosen[:, :, :, :].rearrange("p k g e -> p (k g) e"), AX.X))
            ts(slot_q[:, :], slot[:, :], 1.0 / P, -HALF_DOWN, ALU.mult, ALU.add)
            ts(slot_q[:, :], slot_q[:, :], ROUND, ROUND, ALU.add, ALU.subtract)
            stt(slot[:, :], slot_q[:, :], -float(P), slot[:, :], ALU.mult, ALU.add)
            at_q = slot_tile[:, :, 0:MC]
            col = [P, K * G, MC]
            tt(slot_row, slot[:, :].unsqueeze(2).to_broadcast([P, K * G, P]),
               iota_row[:, :].unsqueeze(1).to_broadcast([P, K * G, P]), ALU.is_equal)
            tt(at_q, slot_q[:, :].unsqueeze(2).to_broadcast(col),
               iota_row[:, 0:MC].unsqueeze(1).to_broadcast(col), ALU.is_equal)
            tt(slot_tile[:, :, MC:], at_q, weight[:, :, :].rearrange("p k g -> p (k g)").unsqueeze(2).to_broadcast(col),
               ALU.mult)
            nc.vector.tensor_tensor(at_q, at_q, token_no[:, :].unsqueeze(2).to_broadcast(col),
                                    ALU.mult).then_inc(slots_made, 1)
            tt(passed[:, :, :], iota_row[:, 0:MC].unsqueeze(2).to_broadcast([P, MC, E]),
               ends[:, :].unsqueeze(1).to_broadcast([P, MC, E]), ALU.is_ge)
            link(nc.vector.reduce_sum(tile_e[:, :], passed[:, :, :], AX.X))
            ts(tile_e[:, :], tile_e[:, :], float(E - 1), None, ALU.min, ALU.bypass)
            ts(tile_f[:, 1, :], tile_e[:, :], 1.0, None, ALU.add, ALU.bypass)
            ts(tile_f[:, 0, :], tile_e[:, :], 1.0 / WB, -(WB - 1) / (2.0 * WB), ALU.mult, ALU.add)
            ts(tile_f[:, 0, :], tile_f[:, 0, :], ROUND, ROUND, ALU.add, ALU.subtract)
            stt(tile_f[:, 0, :], tile_f[:, 0, :], -float(WB), tile_e[:, :], ALU.mult, ALU.add)
            nc.vector.tensor_copy(tile_i[:, :, :], tile_f[:, :, :]).then_inc(experts_made, 1)
            dve.wait_ge(table_made, 1)
            ts(shift[:, :], table_ps[:, 0:MC], 0.0, float(NONE), ALU.is_equal, ALU.mult)
            stt(named[:, :], table_ps[:, 0:MC], -1.0, shift[:, :], ALU.add, ALU.add)
            link(nc.vector.tensor_copy(to_row[:, :], named[:, :]))
            ts(shift[:, :], named[:, :], float(TOK), -float(TOK), ALU.is_ge, ALU.mult)
            tt(named[:, :], named[:, :], shift[:, :], ALU.add)
            link(nc.vector.tensor_copy(slot_weight[:, :], table_ps[:, MC:]))
            nc.vector.tensor_copy(from_row[:, :], named[:, :]).then_inc(lists_made, 1)

            def turn_rest(t, p, first):
                dve.wait_ge(turned, t + 1)
                if not first:
                    dve.wait_ge(gu_done, t - 1)
                nc.vector.tensor_copy(ys_t[:, p, C // 2:, :], ytr_ps[:, L // 2:].rearrange("p (c n) -> p c n", n=P)
                                      ).then_inc(yst_dve, 1)

            def hidden(t, p, first):
                dve.wait_ge(silu_made, t + 1)
                if not first:
                    dve.wait_ge(hid_turned, t - 1)
                nc.vector.tensor_tensor(hid[:, p, :], silu[:, p, :], gu_ps[:, INTER:], ALU.mult).then_inc(hid_made, 1)

            def hidden_turned(t, p, first):
                dve.wait_ge(hid_turned, t + 1)
                if not first:
                    dve.wait_ge(down_done, t - 1)
                nc.vector.tensor_copy(hid_t[:, p, :], hid_ps).then_inc(hid_read, 1)

            def weight_of(t, p, first):
                if not first:
                    dve.wait_ge(od_act, t - 1)
                    dve.wait_ge(od_dve, t - 1)
                nc.vector.tensor_copy(weight_now[:, p:p + 1], slot_weight[:, bass.ds(t, 1)]).then_inc(weight_copied, 1)

            def weigh_rest(t, p, i, first):
                dve.wait_ge(down_done, t + 1)
                dve.wait_ge(weight_copied, t + 1)
                if not first:
                    dve.wait_ge(scattered[p], 16 * i)
                nc.vector.tensor_scalar(od[:, p, L // 2:], down_ps[:, 1, :], weight_now[:, p:p + 1], None,
                                        ALU.mult, ALU.bypass).then_inc(od_dve, 1)

            turn_rest(0, 0, True)
            weight_of(0, 0, True)
            hidden(0, 0, True)
            turn_rest(1, 1, True)
            hidden_turned(0, 0, True)
            weight_of(1, 1, True)
            hidden(1, 1, True)
            turn_rest(2, 0, False)
            weigh_rest(0, 0, 0, True)
            hidden_turned(1, 1, True)
            weight_of(2, 0, False)
            hidden(2, 0, False)
            turn_rest(3, 1, False)
            weigh_rest(1, 1, 0, True)
            hidden_turned(2, 0, False)
            with dve.Fori(1, (MT - 3) // 2) as i:
                for p in (1, 0):
                    weight_of(2 * i + 2 - p, p, False)
                    hidden(2 * i + 2 - p, p, False)
                    turn_rest(2 * i + 3 - p, 1 - p, False)
                    weigh_rest(2 * i + 1 - p, 1 - p, i, False)
                    hidden_turned(2 * i + 2 - p, p, False)
            for t in range(MT - 2, MT):
                weight_of(t, t % 2, False)
                hidden(t, t % 2, False)
                if t + 1 < MT:
                    turn_rest(t + 1, (t + 1) % 2, False)
                weigh_rest(t - 1, (t - 1) % 2, (t - 1) // 2, False)
                hidden_turned(t, t % 2, False)
            weigh_rest(MT - 1, (MT - 1) % 2, (MT - 1) // 2, False)

            dve.wait_ge(x_in, 16 * G)
            for g in range(G):
                dve.wait_ge(pair_in[g % OB], 16 * (g // OB + 1))
                link(nc.vector.tensor_tensor(pair[:, g % OB, 0, :], pair[:, g % OB, 0, :], pair[:, g % OB, 1, :],
                                             ALU.add))
                link(nc.vector.tensor_tensor(arena[:, g, :], arena[:, g, :], pair[:, g % OB, 0, :], ALU.add))
                dve.sem_inc(pair_sum, 1)
                dve.sem_inc(out_made, 1)

        @block.tensor
        def _(pe):
            def products(g, p, first):
                pe.wait_ge(factors_made, g + 1)
                if not first:
                    pe.wait_ge(k_copied, g)
                for h in range(HG):
                    last = nc.tensor.matmul(k_ps[:, h, :], am[:, p, h, :], bm[:, p, h, :], start=True, stop=True)
                last.then_inc(k_made, 1)

            def convolve(g, p, i, first):
                pe.wait_ge(toep_in[p], 16 * (i + 1))
                pe.wait_ge(u_in[p], 16 * (i + 1))
                for h in range(HG):
                    if not first:
                        pe.wait_ge(conv_read, g * HG + h - HG + 1)
                    for d in range(C):
                        last = nc.tensor.matmul(conv_ps[:, h, d * B:C * B], toep[:, p, h, d * P:(d + 1) * P],
                                                u_t[:, p, h, 0:(C - d) * B], start=(d == 0), stop=(d == C - 1))
                    last.then_inc(conv_done, 1)

            def post(g, p, first):
                pe.wait_ge(conv_read, g * HG + HG)
                if not first:
                    pe.wait_ge(log_read, g)
                    pe.wait_ge(ytr_read, g)
                for c in range(C):
                    nc.tensor.matmul(log_ps[:, :], y_t[:, p, c, :], gate_sb[:, c, :], start=(c == 0), stop=(c == C - 1))
                for c in range(C):
                    last = nc.tensor.transpose(ytr_ps[:, c * P:(c + 1) * P], y_t[:, p, c, :], ident[:, :])
                last.then_inc(post_done, 1)

            pe.wait_ge(gate_in, 16)
            pe.wait_ge(consts_made, 1)
            for g in range(3):
                products(g, g % 2, g == 0)
            convolve(0, 0, 0, True)
            products(3, 1, False)
            convolve(1, 1, 0, False)
            post(0, 0, True)
            products(4, 0, False)
            with pe.Fori(1, (G - 4) // 2) as i:
                for p in range(2):
                    convolve(2 * i + p, p, i, False)
                    post(2 * i + p - 1, 1 - p, False)
                    products(2 * i + 3 + p, 1 - p, False)
            for g in range(G - 4, G):
                convolve(g, g % 2, g // 2, False)
                post(g - 1, (g - 1) % 2, False)
                if g + 3 < G:
                    products(g + 3, (g + 3) % 2, False)
            post(G - 1, (G - 1) % 2, False)

            pe.wait_ge(chosen_made, 1)
            nc.tensor.matmul(before_ps, before[:, :], both[:, :, :], start=True, stop=True)
            nc.tensor.matmul(count_ps, ones[:, :], both[:, :, :], start=True, stop=True).then_inc(counted, 1)
            pe.wait_ge(slots_made, 1)
            for j in range(K * G):
                last = nc.tensor.matmul(table_ps, slot_row[:, j, :], slot_tile[:, j, :],
                                        start=(j == 0), stop=(j == K * G - 1))
            last.then_inc(table_made, 1)

            def gate_up(t, p):
                buf = pe.value_load(tile_i[0:1, 0, bass.ds(t, 1)], min_val=0, max_val=WB - 1)
                need = pe.value_load(tile_i[0:1, 1, bass.ds(t, 1)], min_val=1, max_val=E)
                pe.wait_ge(weights_ready, need)
                pe.wait_ge(yst_act, t + 1)
                pe.wait_ge(yst_dve, t + 1)
                for c in range(C):
                    last = nc.tensor.matmul(gu_ps, ys_t[:, p, c, :], w_gu[:, bass.ds(buf * (C * GU) + c * GU, GU)],
                                            start=(c == 0), stop=(c == C - 1))
                last.then_inc(gu_done, 1)

            def turn(t, p, i):
                pe.wait_ge(gathered[p], 16 * (i + 1))
                for c in range(C):
                    last = nc.tensor.transpose(ytr_ps[:, c * P:(c + 1) * P], ys[:, p, c * P:(c + 1) * P], ident[:, :])
                last.then_inc(turned, 1)

            def down(t, p, first):
                buf = pe.value_load(tile_i[0:1, 0, bass.ds(t, 1)], min_val=0, max_val=WB - 1)
                pe.wait_ge(hid_read, t + 1)
                if not first:
                    pe.wait_ge(od_act, t)
                    pe.wait_ge(od_dve, t)
                for n in range(2):
                    last = nc.tensor.matmul(down_ps[:, n, :], hid_t[:, p, :],
                                            w_d[:, bass.ds(buf * L + n * (L // 2), L // 2)], start=True, stop=True)
                last.then_inc(down_done, 1)

            def turn_hidden(t, p):
                pe.wait_ge(hid_made, t + 1)
                nc.tensor.transpose(hid_ps, hid[:, p, :], ident[:, :]).then_inc(hid_turned, 1)

            pe.wait_ge(experts_made, 1)
            pe.wait_ge(lists_made, 1)
            turn(0, 0, 0)
            gate_up(0, 0)
            turn(1, 1, 0)
            turn_hidden(0, 0)
            gate_up(1, 1)
            turn(2, 0, 1)
            down(0, 0, True)
            turn_hidden(1, 1)
            gate_up(2, 0)
            turn(3, 1, 1)
            down(1, 1, False)
            turn_hidden(2, 0)
            with pe.Fori(1, (MT - 3) // 2) as i:
                for p in (1, 0):
                    gate_up(2 * i + 2 - p, p)
                    turn(2 * i + 3 - p, 1 - p, i + 1)
                    down(2 * i + 1 - p, 1 - p, False)
                    turn_hidden(2 * i + 2 - p, p)
            for t in range(MT - 2, MT):
                gate_up(t, t % 2)
                if t + 1 < MT:
                    turn(t + 1, (t + 1) % 2, (t + 1) // 2)
                down(t - 1, (t - 1) % 2, False)
                turn_hidden(t, t % 2)
            down(MT - 1, (MT - 1) % 2, False)


def kernel(x, itok_B_8_3872, L0_cond_log_dt, L0_cond_C, L0_cond_log_A_real, L0_cond_A_imag, L0_cond_D,
           L0_ffn_gate_w, L0_ffn_u, L0_ffn_g, L0_ffn_d):
    import numpy as np
    import concourse.bacc as bacc
    from concourse.bass_utils import run_bass_kernel_spmd

    x = np.asarray(x)
    c = np.asarray(L0_cond_C)
    gu = np.stack([np.asarray(L0_ffn_g), np.asarray(L0_ffn_u)]).reshape(2, E, INTER, C, P)
    arrays = {
        "x_time": x.reshape(B, H, C, P)[:, :, :, ::-1].transpose(3, 1, 2, 0).reshape(P, H, C * B),
        "x_rows": x.transpose(1, 0, 2).reshape(TOK, L),
        "lengths": np.asarray(itok_B_8_3872),
        "log_dt": np.asarray(L0_cond_log_dt),
        "c_re": c[:, :, 0].T,
        "c_im": c[:, :, 1].T,
        "log_a": np.asarray(L0_cond_log_A_real).T,
        "a_im": np.asarray(L0_cond_A_imag).T,
        "skip": np.asarray(L0_cond_D).reshape(1, H),
        "gate_t": np.asarray(L0_ffn_gate_w).reshape(E, C, P).transpose(2, 1, 0),
        "gu_t": gu.transpose(1, 4, 3, 0, 2).reshape(E, P, C * 2 * INTER),
        "d_t": np.asarray(L0_ffn_d).reshape(L, E, INTER).transpose(1, 2, 0),
    }
    arrays = {name: np.ascontiguousarray(a) for name, a in arrays.items()}
    nc = bacc.Bacc("TRN2", target_bir_lowering=False, num_devices=1)
    ins = [nc.dram_tensor(name, a.shape, mybir.dt.from_np(a.dtype), kind="ExternalInput").ap()
           for name, a in arrays.items()]
    out = nc.dram_tensor("out", (TOK, L), mybir.dt.float32, kind="ExternalOutput").ap()
    build(nc, *ins, out)
    got = run_bass_kernel_spmd(nc, [arrays], core_ids=[0]).results[0]["out"]
    return np.ascontiguousarray(got.reshape(H, B, L).transpose(1, 0, 2))
```

```python
import math
from contextlib import ExitStack

import concourse.bass as bass
from concourse import mybir

B, H, L = 32, 64, 1024
N = 64
P = 128
E, INTER, K = 16, 112, 2
TOK = B * H
C = L // P
HG = P // B
G = H // HG
LO = 32
SEG = 3 * LO
KROW = L + P
MT = -(-K * TOK // P) + E - 1

LOG2E = 1.0 / math.log(2.0)
LN2_HI = 0.693359375
LN2_LO = math.log(2.0) - LN2_HI
TWO_PI = 2.0 * math.pi
TWO_PI_HI = 6.28125
TWO_PI_MID = round((TWO_PI - TWO_PI_HI) * 2**20) / 2**20
TWO_PI_LO = TWO_PI - TWO_PI_HI - TWO_PI_MID
ROUND = 1.5 * 2.0**23
PI_IN = 3.1415925
EXP_TERMS = 7
GU = 2 * INTER
LEAST = K * TOK // P
MC = MT + 1
WB = 4
PIECES = ((0, 4), (4, 8), (8, 16), (16, 24), (24, K * G))
NONE = 4 * K * TOK
HALF_DOWN = (P - 1) / (2.0 * P)


def build(nc, x_time, x_rows, lengths, params, skip, gate_t, gu_t, d_t, out):
    fp32, i32, u32 = mybir.dt.float32, mybir.dt.int32, mybir.dt.uint32
    ALU, ACT, AX = mybir.AluOpType, mybir.ActivationFunctionType, mybir.AxisListType

    ctx = ExitStack()
    with ctx:
        def sb(name, shape, dt=fp32):
            return ctx.enter_context(nc.sbuf_tensor(name, shape, dt))

        def pb(name, shape, dt=fp32):
            return ctx.enter_context(nc.psum_tensor(name, shape, dt))

        def sem(name):
            return ctx.enter_context(nc.semaphore(name))

        k_rows = nc.dram_tensor("k_rows", [H, KROW], fp32)
        y_rows = nc.dram_tensor("y_rows", [TOK, L], fp32).ap()

        flat = sb("arena", [P, 2 * HG * L + H * 2 * LO + 2 * HG * C * B + 2 * C * P])
        toep = flat[:, 0:2 * HG * L].rearrange("p (s h l) -> p s h l", s=2, h=HG)
        at = 2 * HG * L
        mag = flat[:, at:at + H * 2 * LO].rearrange("p (h l) -> p h l", h=H)
        at += H * 2 * LO
        u_t = flat[:, at:at + 2 * HG * C * B].rearrange("p (s h n) -> p s h n", s=2, h=HG)
        at += 2 * HG * C * B
        y_t = flat[:, at:at + 2 * C * P].rearrange("p (s c n) -> p s c n", s=2, c=C)
        slot_row = flat[:, 0:K * G * P].rearrange("p (j r) -> p j r", j=K * G)
        slot_hot = flat[:, K * G * (P + 2 * MC):K * G * (P + 3 * MC)].rearrange("p (j n) -> p j n", j=K * G)
        slot_tile = flat[:, K * G * P:K * G * (P + 2 * MC)].rearrange("p (j n) -> p j n", j=K * G)
        par = sb("par", [P, 5, H])
        LOGDT, LOGA, AIM, CRE, CIM = range(5)
        skip_row = sb("skip_row", [1, H])
        tmp = sb("tmp", [P, 24, H])
        tmp_i = sb("tmp_i", [P, 2, H], i32)
        decay = sb("decay", [P, H])
        omega = sb("omega", [P, H])
        cs_re = sb("cs_re", [P, H])
        cs_im = sb("cs_im", [P, H])
        steps = sb("steps", [P, SEG])
        off_turns = sb("off_turns", [P, SEG])
        off_rad = sb("off_rad", [P, SEG])
        phase = sb("phase", [P, 2, HG, SEG])
        turns = sb("turns", [P, 2, HG, SEG])
        angle = sb("angle", [P, 2, HG, SEG])
        wave = sb("wave", [P, 2, HG, SEG])
        am = sb("am", [P, 2, HG, LO])
        am2 = sb("am2", [P, 2, HG, LO])
        bm = sb("bm", [P, 2, HG, LO])
        k_sb = sb("k_sb", [LO, 2, HG, LO])
        zero = sb("zero", [H, P])
        y_tok = sb("y_tok", [P, 2, L])
        mask_t = sb("mask_t", [P, C, B])
        len_i = sb("len_i", [P, B], i32)
        len_f = sb("len_f", [P, B])
        time_col = sb("time_col", [P, C])
        ident = sb("ident", [P, P])
        gate_sb = sb("gate_sb", [P, C, E])
        logits = sb("logits", [P, G, E])
        top_v = sb("top_v", [P, G, 8])
        top_i = sb("top_i", [P, G, 8], u32)

        iota_row = sb("iota_row", [P, P])
        not_before = sb("not_before", [P, P])
        ones = sb("ones", [P, P])
        token_no = sb("token_no", [P, K * G])
        spread = sb("spread", [P, G, E])
        total = sb("total", [P, G])
        top2 = sb("top2", [P, K, G])
        weight = sb("weight", [P, K, G])
        norm = sb("norm", [P, G])
        expert = sb("expert", [P, K, G])
        chosen = sb("chosen", [P, K, G, E])
        both = sb("both", [P, E, G])
        not_first = sb("not_first", [P, E, G])
        run = sb("run", [P, E, G])
        tiles = sb("tiles", [P, E])
        ends = sb("ends", [P, E])
        starts = sb("starts", [P, E])
        dest = sb("dest", [P, E, G])
        slot = sb("slot", [P, K * G])
        slot_q = sb("slot_q", [P, K * G])
        named = sb("named", [P, MC])
        shift = sb("shift", [P, MC])
        slot_weight = sb("slot_weight", [P, MC])
        spare = sb("spare", [P, 1])
        from_row = sb("from_row", [P, MC], i32)
        to_row = sb("to_row", [P, MC], i32)
        passed = sb("passed", [P, MC, E])
        tile_e = sb("tile_e", [P, MC])
        tile_f = sb("tile_f", [P, 2, MC])
        tile_i = sb("tile_i", [P, 2, MC], i32)
        ends_i = sb("ends_i", [P, E], i32)

        w_gu = sb("w_gu", [P, WB * C * GU])
        w_d = sb("w_d", [INTER, WB * L])
        ys = sb("ys", [P, 2, L])
        ys_t = sb("ys_t", [P, 2, C, P])
        weight_now = sb("weight_now", [P, 2])
        silu = sb("silu", [P, 2, INTER])
        hid = sb("hid", [P, 2, INTER])
        hid_t = sb("hid_t", [INTER, 2, P])
        od = sb("od", [P, 2, L])

        conv_ps = pb("conv_ps", [P, HG, 512])
        k_ps = pb("k_ps", [LO, HG, LO])
        later_ps = conv_ps[:, 0, 0:E * G].rearrange("p (e g) -> p e g", e=E)
        count_ps = conv_ps[:, 1, 0:E * G].rearrange("p (e g) -> p e g", e=E)
        table_ps = conv_ps[:, 2, 0:2 * MC]
        down_ps = conv_ps[:, 0:2, :]
        gu_ps = conv_ps[:, 2, 0:GU]
        hid_ps = conv_ps[0:INTER, 3, 0:P]
        log_ps = pb("log_ps", [P, P])
        ytr_ps = pb("ytr_ps", [P, L])

        par_in = sem("par_in")
        len_in = sem("len_in")
        gate_in = sem("gate_in")
        ys_cleared = sem("ys_cleared")
        x_copied = sem("x_copied")
        spare_out = sem("spare_out")
        zero_made = sem("zero_made")
        pads_out = sem("pads_out")
        chain = sem("chain")
        act_chain = sem("act_chain")
        pool_chain = sem("pool_chain")
        half_sin = sem("half_sin")
        trig_in = sem("trig_in")
        decay_made = sem("decay_made")
        omega_made = sem("omega_made")
        square_made = sem("square_made")
        coef_made = sem("coef_made")
        consts_made = sem("consts_made")
        mask_ready = sem("mask_ready")
        growth_made = sem("growth_made")
        mag_made = sem("mag_made")
        phase_made = sem("phase_made")
        angle_steps = sem("angle_steps")
        angle_made = sem("angle_made")
        wave_made = sem("wave_made")
        am_steps = sem("am_steps")
        factors_made = sem("factors_made")
        k_made = sem("k_made")
        k_copied = sem("k_copied")
        k_added = sem("k_added")
        k_stored = [sem(f"k_stored{i}") for i in range(2)]
        toep_in = [sem(f"toep_in{i}") for i in range(2)]
        toep_first = [[sem(f"toep_first{p}_{h}") for h in range(HG)] for p in range(2)]
        u_in = [sem(f"u_in{i}") for i in range(2)]
        conv_done = sem("conv_done")
        conv_read = sem("conv_read")
        log_done = sem("log_done")
        post_done = sem("post_done")
        ytr_read = sem("ytr_read")
        log_read = sem("log_read")
        top_made = sem("top_made")
        y_stored = [sem(f"y_stored{i}") for i in range(2)]

        starts_marked = sem("starts_marked")
        top_found = sem("top_found")
        spread_made = sem("spread_made")
        spread_exp = sem("spread_exp")
        chosen_made = sem("chosen_made")
        counted = sem("counted")
        hot_made = sem("hot_made")
        hot_row_made = sem("hot_row_made")
        hot_weight_made = sem("hot_weight_made")
        hot_token_made = sem("hot_token_made")
        sources_made = sem("sources_made")
        table_made = sem("table_made")
        lists_made = sem("lists_made")
        experts_made = sem("experts_made")
        ends_made = sem("ends_made")
        weights_ready = sem("weights_ready")
        gu_done = sem("gu_done")
        yst_act = sem("yst_act")
        yst_dve = sem("yst_dve")
        silu_made = sem("silu_made")
        hid_made = sem("hid_made")
        turned = sem("turned")
        hid_turned = sem("hid_turned")
        hid_read = sem("hid_read")
        down_done = sem("down_done")
        od_act = sem("od_act")
        od_dve = sem("od_dve")
        weight_copied = sem("weight_copied")
        w_in = [sem(f"w_in{i}") for i in range(WB)]
        gathered = [sem(f"gathered{i}") for i in range(2)]
        scattered = [sem(f"scattered{i}") for i in range(2)]

        block = ctx.enter_context(nc.Block())

        def tiles_in_use(eng):
            return eng.value_load(ends_i[0:1, E - 1:E], min_val=LEAST, max_val=MT)

        def pairs(eng, used, pair):
            with eng.Fori(1, (LEAST - 1) // 2 + 1) as i:
                pair(i)
            with eng.Fori((LEAST - 1) // 2 + 1, (MT - 3) // 2) as i:
                with eng.If(used >= 2 * i + 1):
                    pair(i)

        def first_step(s):
            return min(s - (s + 1) % 2, MT - 2)

        def hs(g):
            return bass.ds(g * HG, HG)

        @block.sync
        def _(sp):
            sp.dma_start(par[:, :, :], params).then_inc(par_in, 16)
            sp.dma_start(skip_row[:, :], skip).then_inc(par_in, 16)
            sp.dma_start(len_i[:, :], lengths.partition_broadcast(P)).then_inc(len_in, 16)
            sp.dma_start(gate_sb[:, :, :], gate_t).then_inc(gate_in, 16)
            def copy_x(q):
                part = slice(q * (TOK // 4), (q + 1) * (TOK // 4))
                sp.dma_start(out[part, :], x_rows[part, :]).then_inc(x_copied, 16)

            sp.wait_ge(ys_cleared, 1)
            sp.dma_start(out[TOK:, :], ys[:, 0, :]).then_inc(spare_out, 16)
            sp.wait_ge(zero_made, 1)
            sp.dma_start(k_rows.ap()[:, 0:P - 1], zero[:, 0:P - 1]).then_inc(pads_out, 16)
            for q in range(3):
                copy_x(q)
            sp.wait_ge(pads_out, 16)

            def load_expert(e):
                s = e % WB
                sp.dma_start(w_gu[:, s * C * GU:(s + 1) * C * GU], gu_t[e]).then_inc(w_in[s], 16)
                sp.dma_start(w_d[:, s * L:(s + 1) * L], d_t[e]).then_inc(w_in[s], 16)

            for g in range(G):
                p, i = g % 2, g // 2
                sp.wait_ge(k_added, g + 1)
                sp.dma_start(bass.AP(k_rows, g * HG * KROW + P - 1, [[LO, LO], [KROW, HG], [1, LO]]),
                             k_sb[:, p, :, :]).then_inc(k_stored[p], 16)
                if g >= 2:
                    sp.wait_ge(conv_done, (g - 1) * HG)
                sp.dma_start(u_t[:, p, :, :], x_time[:, g * HG:(g + 1) * HG, :]).then_inc(u_in[p], 16)
                sp.wait_ge(k_stored[p], 16 * (i + 1))
                if g < 2:
                    for h in range(HG):
                        sp.dma_start(toep[:, p, h, :], bass.AP(k_rows, (g * HG + h) * KROW, [[1, P], [1, L]])
                                     ).then_inc(toep_first[p][h], 16)
                else:
                    sp.dma_start(toep[:, p, :, :], bass.AP(k_rows, g * HG * KROW, [[1, P], [KROW, HG], [1, L]])
                                 ).then_inc(toep_in[p], 16)
            for e in range(WB):
                load_expert(e)
            copy_x(3)
            for e in range(WB):
                sp.wait_ge(w_in[e % WB], 32)
                sp.sem_inc(weights_ready, 1)
            sp.wait_ge(ends_made, 1)
            sp.wait_ge(lists_made, 1)
            for e in range(WB, E):
                end = sp.value_load(ends_i[0:1, e - WB:e - WB + 1], min_val=1, max_val=MT)
                sp.wait_ge(down_done, end)
                load_expert(e)
                sp.wait_ge(w_in[e % WB], 32 * (e // WB + 1))
                sp.sem_inc(weights_ready, 1)

        @block.gpsimd
        def _(pool):
            made = [0]

            def link(ins):
                made[0] += 1
                ins.then_inc(pool_chain, 1)
                pool.wait_ge(pool_chain, made[0])

            nc.gpsimd.memset(zero[:, :], 0.0).then_inc(zero_made, 1)
            for k, m in ((0, LO), (1, LO), (2, 1)):
                nc.gpsimd.iota(steps[:, k * LO:(k + 1) * LO], [[m, LO]], base=0, channel_multiplier=0,
                               allow_small_or_imprecise_dtypes=True)
            nc.gpsimd.iota(time_col[:, :], [[P, C]], base=0, channel_multiplier=1,
                           allow_small_or_imprecise_dtypes=True)
            nc.gpsimd.iota(iota_row[:, :], [[1, P]], base=0, channel_multiplier=0,
                           allow_small_or_imprecise_dtypes=True)
            nc.gpsimd.iota(token_no[:, :], [[0, K], [P, G]], base=1, channel_multiplier=1,
                           allow_small_or_imprecise_dtypes=True)
            nc.gpsimd.iota(spare[:, :], [[0, 1]], base=TOK + 1, channel_multiplier=1,
                           allow_small_or_imprecise_dtypes=True)
            nc.gpsimd.memset(ys[:, :, :], 0.0).then_inc(ys_cleared, 1)
            nc.gpsimd.memset(ones[:, :], 1.0)
            link(nc.gpsimd.memset(not_before[:, :], 0.0))
            nc.gpsimd.affine_select(out=not_before[:, :], in_=not_before[:, :], compare_op=ALU.is_gt, fill=-1.0,
                                    base=0, pattern=[[1, P]], channel_multiplier=-1)
            link(nc.gpsimd.memset(ident[:, :], 0.0))
            nc.gpsimd.affine_select(out=ident[:, :], in_=ident[:, :], compare_op=ALU.not_equal, fill=1.0,
                                    base=0, pattern=[[-1, P]], channel_multiplier=1).then_inc(consts_made, 1)
            pool.wait_ge(consts_made, 1)
            pool.wait_ge(decay_made, 1)
            def growth(lo, hi):
                nc.gpsimd.tensor_tensor(mag[:, lo:hi, :], decay[:, lo:hi].unsqueeze(2).to_broadcast([P, hi - lo, 2 * LO]),
                                        steps[:, LO:].unsqueeze(1).to_broadcast([P, hi - lo, 2 * LO]),
                                        ALU.mult).then_inc(growth_made, 1)

            growth(0, 2 * HG)

            def phases(g, p, first):
                if not first:
                    pool.wait_ge(angle_made, g - 1)
                nc.gpsimd.tensor_tensor(phase[:, p, :, :],
                                        omega[:, hs(g)].unsqueeze(2).to_broadcast([P, HG, SEG]),
                                        steps[:, :].unsqueeze(1).to_broadcast([P, HG, SEG]),
                                        ALU.mult).then_inc(phase_made, 1)

            def factors(g, p, first):
                pool.wait_ge(wave_made, g + 1)
                if not first:
                    pool.wait_ge(k_made, g - 1)
                bc = [P, HG, LO]
                nc.gpsimd.tensor_tensor(am[:, p, :, :], wave[:, p, :, 0:LO],
                                        cs_re[:, hs(g)].unsqueeze(2).to_broadcast(bc), ALU.mult).then_inc(am_steps, 1)
                nc.gpsimd.tensor_tensor(am2[:, p, :, :], wave[:, p, :, LO:2 * LO],
                                        cs_im[:, hs(g)].unsqueeze(2).to_broadcast(bc), ALU.mult).then_inc(am_steps, 1)
                nc.gpsimd.tensor_tensor(bm[:, p, :, :], wave[:, p, :, 2 * LO:], mag[:, hs(g), LO:],
                                        ALU.mult).then_inc(am_steps, 1)
                pool.wait_ge(am_steps, 4 * g + 3)
                nc.gpsimd.tensor_tensor(am[:, p, :, :], am[:, p, :, :], am2[:, p, :, :], ALU.add).then_inc(am_steps, 1)
                pool.wait_ge(am_steps, 4 * g + 4)
                nc.gpsimd.tensor_tensor(am[:, p, :, :], am[:, p, :, :], mag[:, hs(g), 0:LO],
                                        ALU.mult).then_inc(factors_made, 1)

            pool.wait_ge(omega_made, 1)
            for p in range(2):
                phases(p, p, True)
            link(nc.gpsimd.tensor_tensor(tmp[:, 22, :], tmp[:, 5, :], tmp[:, 5, :], ALU.mult))
            link(nc.gpsimd.tensor_tensor(tmp[:, 23, :], par[:, AIM, :], par[:, AIM, :], ALU.mult))
            nc.gpsimd.tensor_tensor(tmp[:, 22, :], tmp[:, 22, :], tmp[:, 23, :], ALU.add).then_inc(square_made, 1)
            growth(2 * HG, H)
            link(nc.gpsimd.memset(not_first[:, :, :], 1.0))
            nc.gpsimd.memset(not_first[:, :, 0:1], 0.0).then_inc(starts_marked, 1)
            pool.wait_ge(coef_made, 1)
            pool.wait_ge(mag_made, 1)
            for p in range(2):
                factors(p, p, True)
                phases(2 + p, p, False)
            pool.wait_ge(mag_made, 2)
            with pool.Fori(1, G // 2 - 1) as i:
                for p in range(2):
                    factors(2 * i + p, p, False)
                    phases(2 * i + 2 + p, p, False)
            for p in range(2):
                factors(G - 2 + p, p, False)

            weights = weight[:, :, :].rearrange("p k g -> p (k g)")
            for q, (lo, hi) in enumerate(PIECES):
                js = slice(lo, hi)
                pool.wait_ge(hot_made, q + 1)
                nc.gpsimd.tensor_tensor(slot_tile[:, js, 0:MC], slot_hot[:, js, :],
                                        token_no[:, js].unsqueeze(2).to_broadcast([P, hi - lo, MC]),
                                        ALU.mult).then_inc(hot_token_made, 1)
                nc.gpsimd.tensor_tensor(slot_tile[:, js, MC:], slot_hot[:, js, :],
                                        weights[:, js].unsqueeze(2).to_broadcast([P, hi - lo, MC]),
                                        ALU.mult).then_inc(hot_weight_made, 1)

            def gather(t):
                if t >= 2:
                    pool.wait_ge(turned, t - 1)
                nc.gpsimd.indirect_dma_start(
                    out=ys[:, t % 2, :], out_offset=None, in_=y_rows,
                    in_offset=bass.IndirectOffsetOnAxis(ap=from_row[:, t:t + 1], axis=0),
                    bounds_check=TOK - 1, oob_is_err=False).then_inc(gathered[t % 2], 16)

            def scatter(t):
                pool.wait_ge(od_act, t + 1)
                pool.wait_ge(od_dve, t + 1)
                if t >= 1:
                    pool.wait_ge(scattered[(t - 1) % 2], 16 * ((t - 1) // 2 + 1))
                nc.gpsimd.indirect_dma_start(
                    out=out, out_offset=bass.IndirectOffsetOnAxis(ap=to_row[:, t:t + 1], axis=0),
                    in_=od[:, t % 2, :], in_offset=None, compute_op=ALU.add,
                    bounds_check=TOK + P - 1, oob_is_err=True).then_inc(scattered[t % 2], 16)

            pool.wait_ge(sources_made, 1)
            for p in range(2):
                pool.wait_ge(y_stored[p], 16 * (G // 2))
            gather(0)
            gather(1)
            gather(2)
            pool.wait_ge(lists_made, 1)
            pool.wait_ge(x_copied, 4 * 16)
            pool.wait_ge(spare_out, 16)
            used = tiles_in_use(pool)
            for t in range(1, MT + 2):
                if t + 2 < MT:
                    if first_step(t + 1) <= LEAST:
                        gather(t + 2)
                    else:
                        with pool.If(used >= first_step(t + 1)):
                            gather(t + 2)
                if t >= 2:
                    if first_step(t - 1) <= LEAST:
                        scatter(t - 2)
                    else:
                        with pool.If(used >= first_step(t - 1)):
                            scatter(t - 2)
            with pool.If(used >= MT - 2):
                pool.wait_ge(scattered[0], 16 * ((MT + 1) // 2))
                pool.wait_ge(scattered[1], 16 * (MT // 2))
            for p in range(2):
                pool.wait_ge(scattered[p], (used + 1) // 2 * 16)

        @block.scalar
        def _(act):
            act.wait_ge(growth_made, 1)
            nc.scalar.activation(mag[:, 0:2 * HG, :], mag[:, 0:2 * HG, :], ACT.Exp).then_inc(mag_made, 1)
            act.wait_ge(trig_in, 1)
            nc.scalar.activation(tmp[:, 10, :], tmp[:, 9, :], ACT.Sin, scale=0.5)
            nc.scalar.activation(tmp[:, 11, :], tmp[:, 9, :], ACT.Sin).then_inc(half_sin, 1)

            def waves(g, p, first):
                act.wait_ge(angle_made, g + 1)
                if not first:
                    act.wait_ge(factors_made, g - 1)
                nc.scalar.activation(wave[:, p, :, :], angle[:, p, :, :], ACT.Sin).then_inc(wave_made, 1)

            def rows_out(g, p, i, first):
                act.wait_ge(post_done, g + 1)
                if not first:
                    act.wait_ge(y_stored[p], 16 * i)
                nc.scalar.copy(y_tok[:, p, :], ytr_ps[:, :]).then_inc(ytr_read, 1)
                act.wait_ge(ytr_read, g + 1)
                act.dma_start(y_rows[bass.ds(g * P, P), :], y_tok[:, p, :]).then_inc(y_stored[p], 16)

            for g in range(2):
                waves(g, g % 2, True)
            act.wait_ge(growth_made, 2)
            nc.scalar.activation(mag[:, 2 * HG:, :], mag[:, 2 * HG:, :], ACT.Exp).then_inc(mag_made, 1)
            for g in range(2, 5):
                waves(g, g % 2, False)
            for p in range(2):
                rows_out(p, p, 0, True)
                waves(5 + p, 1 - p, False)
            with act.Fori(1, (G - 6) // 2) as i:
                for p in range(2):
                    rows_out(2 * i + p, p, i, False)
                    waves(2 * i + 5 + p, 1 - p, False)
            for g in range(G - 6, G):
                rows_out(g, g % 2, g // 2, False)
                if g + 5 < G:
                    waves(g + 5, (g + 5) % 2, False)

            act.wait_ge(spread_made, 2)
            nc.scalar.activation(spread[:, :, :], spread[:, :, :], ACT.Exp)
            nc.scalar.activation(top2[:, :, :], top2[:, :, :], ACT.Exp).then_inc(spread_exp, 1)
            nc.scalar.activation(silu[:, 0, 0:1], len_f[:, 0:1], ACT.Silu)

            def turn_half(t, p, first):
                act.wait_ge(turned, t + 1)
                if not first:
                    act.wait_ge(gu_done, t - 1)
                nc.scalar.copy(ys_t[:, p, 0:C // 2, :], ytr_ps[:, 0:L // 2].rearrange("p (c n) -> p c n", n=P)
                               ).then_inc(yst_act, 1)

            def gate(t, p, first):
                act.wait_ge(gu_done, t + 1)
                if not first:
                    act.wait_ge(hid_made, t - 1)
                nc.scalar.activation(silu[:, p, :], gu_ps[:, 0:INTER], ACT.Silu).then_inc(silu_made, 1)

            def weigh_half(t, p, i, first):
                act.wait_ge(down_done, t + 1)
                act.wait_ge(weight_copied, t + 1)
                if not first:
                    act.wait_ge(scattered[p], 16 * i)
                nc.scalar.mul(od[:, p, 0:L // 2], down_ps[:, 0, :], weight_now[:, p:p + 1]).then_inc(od_act, 1)

            turn_half(0, 0, True)
            gate(0, 0, True)
            turn_half(1, 1, True)
            gate(1, 1, True)
            turn_half(2, 0, False)
            weigh_half(0, 0, 0, True)
            gate(2, 0, False)
            turn_half(3, 1, False)
            weigh_half(1, 1, 0, True)

            def pair(i):
                for p in (1, 0):
                    gate(2 * i + 2 - p, p, False)
                    turn_half(2 * i + 3 - p, 1 - p, False)
                    weigh_half(2 * i + 1 - p, 1 - p, i, False)

            act.wait_ge(ends_made, 1)
            used = tiles_in_use(act)
            pairs(act, used, pair)
            with act.If(used >= MT - 2):
                for t in range(MT - 2, MT):
                    gate(t, t % 2, False)
                    if t + 1 < MT:
                        turn_half(t + 1, (t + 1) % 2, False)
                    weigh_half(t - 1, (t - 1) % 2, (t - 1) // 2, False)
                weigh_half(MT - 1, (MT - 1) % 2, (MT - 1) // 2, False)

        @block.vector
        def _(dve):
            made = [0]

            def link(ins):
                made[0] += 1
                ins.then_inc(chain, 1)
                dve.wait_ge(chain, made[0])

            def tt(out, a, b, op):
                link(nc.vector.tensor_tensor(out, a, b, op))

            def ts(out, a, s1, s2, op0, op1):
                link(nc.vector.tensor_scalar(out, a, s1, s2, op0, op1))

            def stt(out, a, s, b, op0, op1):
                link(nc.vector.scalar_tensor_tensor(out, a, s, b, op0, op1))

            def t(i, n=1):
                return tmp[:, i, :] if n == 1 else tmp[:, i:i + n, :]

            for part, quarters in ((0, (1, 2, 1)), (1, (2, -1, 0))):
                for k, q in enumerate(quarters):
                    rows, cols = slice(part * N, part * N + N), slice(k * LO, (k + 1) * LO)
                    link(nc.vector.memset(off_turns[rows, cols], q * 0.25))
                    link(nc.vector.memset(off_rad[rows, cols], q * 0.25 * TWO_PI))
            dve.wait_ge(par_in, 32)
            logs = par[:, LOGDT:LOGA + 1, :]
            k2, r2, p2 = t(0, 2), t(2, 2), t(4, 2)
            ts(k2, logs, LOG2E, ROUND, ALU.mult, ALU.add)
            ts(k2, k2, ROUND, -126.0, ALU.subtract, ALU.max)
            stt(r2, k2, -LN2_HI, logs, ALU.mult, ALU.add)
            stt(r2, k2, -LN2_LO, r2, ALU.mult, ALU.add)
            ts(p2, r2, 1.0 / math.factorial(EXP_TERMS), None, ALU.mult, ALU.bypass)
            for n in range(EXP_TERMS - 1, 0, -1):
                stt(p2, p2, 1.0 / math.factorial(n), r2, ALU.add, ALU.mult)
            ts(tmp_i[:, :, :], k2, 127.0, 2.0**23, ALU.add, ALU.mult)
            stt(p2, p2, 1.0, tmp_i[:, :, :].bitcast(fp32), ALU.add, ALU.mult)
            dt, a_abs, a_imag = t(4), t(5), par[:, AIM, :]
            link(nc.vector.scalar_tensor_tensor(decay[:, :], a_abs, -1.0, dt, ALU.mult, ALU.mult))
            nc.vector.tensor_tensor(omega[:, :], a_imag, dt, ALU.mult).then_inc(omega_made, 1)
            dve.wait_ge(omega_made, 1)
            dve.sem_inc(decay_made, 1)
            ts(t(8), omega[:, :], 1.0 / TWO_PI, ROUND, ALU.mult, ALU.add)
            ts(t(8), t(8), ROUND, None, ALU.subtract, ALU.bypass)
            stt(t(9), t(8), -TWO_PI_HI, omega[:, :], ALU.mult, ALU.add)
            stt(t(9), t(8), -TWO_PI_MID, t(9), ALU.mult, ALU.add)
            stt(t(9), t(8), -TWO_PI_LO, t(9), ALU.mult, ALU.add)
            nc.vector.tensor_scalar(t(9), t(9), PI_IN, -PI_IN, ALU.min, ALU.max).then_inc(trig_in, 1)
            def angles(g, p, first):
                dve.wait_ge(phase_made, g + 1)
                off_t = off_turns[:, :].unsqueeze(1).to_broadcast([P, HG, SEG])
                off_r = off_rad[:, :].unsqueeze(1).to_broadcast([P, HG, SEG])
                ph, tu, an = phase[:, p, :, :], turns[:, p, :, :], angle[:, p, :, :]
                nc.vector.scalar_tensor_tensor(tu, ph, 1.0 / TWO_PI, off_t, ALU.mult, ALU.add).then_inc(angle_steps, 1)
                dve.wait_ge(angle_steps, 6 * g + 1)
                nc.vector.tensor_scalar(tu, tu, ROUND, ROUND, ALU.add, ALU.subtract).then_inc(angle_steps, 1)
                dve.wait_ge(angle_steps, 6 * g + 2)
                if not first:
                    dve.wait_ge(wave_made, g - 1)
                nc.vector.scalar_tensor_tensor(an, tu, -TWO_PI_HI, ph, ALU.mult, ALU.add).then_inc(angle_steps, 1)
                dve.wait_ge(angle_steps, 6 * g + 3)
                nc.vector.scalar_tensor_tensor(an, tu, -TWO_PI_MID, an, ALU.mult, ALU.add).then_inc(angle_steps, 1)
                dve.wait_ge(angle_steps, 6 * g + 4)
                nc.vector.scalar_tensor_tensor(an, tu, -TWO_PI_LO, an, ALU.mult, ALU.add).then_inc(angle_steps, 1)
                dve.wait_ge(angle_steps, 6 * g + 5)
                nc.vector.tensor_tensor(an, an, off_r, ALU.add).then_inc(angle_steps, 1)
                dve.wait_ge(angle_steps, 6 * g + 6)
                nc.vector.tensor_scalar(an, an, PI_IN, -PI_IN, ALU.min, ALU.max).then_inc(angle_made, 1)

            angles(0, 0, True)
            ts(t(12), decay[:, :], -20.0, 1.0 / 16.0, ALU.max, ALU.mult)
            ts(t(13), t(12), 1.0 / math.factorial(EXP_TERMS), None, ALU.mult, ALU.bypass)
            for n in range(EXP_TERMS - 1, 0, -1):
                stt(t(13), t(13), 1.0 / math.factorial(n), t(12), ALU.add, ALU.mult)
            for n in range(4):
                stt(t(13), t(13), 2.0, t(13), ALU.add, ALU.mult)
            dve.wait_ge(square_made, 1)
            link(nc.vector.reciprocal(t(22), t(22)))
            dve.wait_ge(half_sin, 1)
            stt(t(14), t(10), 2.0, t(10), ALU.mult, ALU.mult)
            ts(t(15), t(14), -1.0, 1.0, ALU.mult, ALU.add)
            tt(t(15), t(15), t(13), ALU.mult)
            tt(t(15), t(15), t(14), ALU.subtract)
            stt(t(16), t(13), 1.0, t(11), ALU.add, ALU.mult)
            cre, cim = par[:, CRE, :], par[:, CIM, :]
            tt(t(17), cre, t(15), ALU.mult)
            tt(t(18), cim, t(16), ALU.mult)
            tt(t(17), t(17), t(18), ALU.subtract)
            tt(t(18), cre, t(16), ALU.mult)
            tt(t(19), cim, t(15), ALU.mult)
            tt(t(18), t(18), t(19), ALU.add)
            tt(t(20), t(18), a_imag, ALU.mult)
            tt(t(21), t(17), a_abs, ALU.mult)
            tt(t(20), t(20), t(21), ALU.subtract)
            stt(cs_re[:, :], t(20), 2.0, t(22), ALU.mult, ALU.mult)
            tt(t(20), t(18), a_abs, ALU.mult)
            tt(t(21), t(17), a_imag, ALU.mult)
            tt(t(20), t(20), t(21), ALU.add)
            nc.vector.scalar_tensor_tensor(cs_im[:, :], t(20), -2.0, t(22), ALU.mult, ALU.mult).then_inc(coef_made, 1)

            def kernel_rows(g, p, i, first):
                dve.wait_ge(k_made, g + 1)
                if not first:
                    dve.wait_ge(k_stored[p], 16 * i)
                nc.vector.tensor_copy(k_sb[:, p, :, :], k_ps[:, :, :]).then_inc(k_copied, 1)
                dve.wait_ge(k_copied, g + 1)
                nc.vector.tensor_tensor(k_sb[0:1, p, :, 0], k_sb[0:1, p, :, 0], skip_row[0:1, hs(g)],
                                        ALU.add).then_inc(k_added, 1)

            def outputs(g, p, first):
                if not first:
                    dve.wait_ge(post_done, g - 1)
                for h in range(HG):
                    dve.wait_ge(conv_done, g * HG + h + 1)
                    nc.vector.tensor_tensor(y_t[:, p, :, h * B:(h + 1) * B],
                                            conv_ps[:, h, 0:C * B].rearrange("p (c b) -> p c b", c=C),
                                            mask_t[:, :, :], ALU.mult).then_inc(conv_read, 1)

            def router(g):
                dve.wait_ge(log_done, g + 1)
                nc.vector.tensor_copy(logits[:, bass.ds(g, 1), :], log_ps[:, 0:E].unsqueeze(1)).then_inc(log_read, 1)

            def choose(lo, hi):
                for g in range(lo, hi):
                    nc.vector.max(top_v[:, g, :], logits[:, g, :]).then_inc(top_found, 1)
                dve.wait_ge(top_found, hi)
                for g in range(lo, hi):
                    nc.vector.max_index(top_i[:, g, :], top_v[:, g, :], logits[:, g, :]).then_inc(top_made, 1)
                dve.wait_ge(top_made, hi)
                n = hi - lo
                link(nc.vector.tensor_copy(expert[:, :, lo:hi], top_i[:, lo:hi, 0:K].rearrange("p g k -> p k g")))
                for k in range(K):
                    tt(chosen[:, k, lo:hi, :], expert[:, k, lo:hi].unsqueeze(2).to_broadcast([P, n, E]),
                       iota_row[:, 0:E].unsqueeze(1).to_broadcast([P, n, E]), ALU.is_equal)
                nc.vector.tensor_tensor(both[:, :, lo:hi].rearrange("p e g -> p g e"), chosen[:, 0, lo:hi, :],
                                        chosen[:, 1, lo:hi, :], ALU.add).then_inc(chosen_made, 1)
                tt(spread[:, lo:hi, :], logits[:, lo:hi, :], top_v[:, lo:hi, 0:1].to_broadcast([P, n, E]), ALU.subtract)
                nc.vector.tensor_tensor(top2[:, :, lo:hi], top_v[:, lo:hi, 0:K].rearrange("p g k -> p k g"),
                                        top_v[:, lo:hi, 0].unsqueeze(1).to_broadcast([P, K, n]),
                                        ALU.subtract).then_inc(spread_made, 1)

            dve.wait_ge(len_in, 16)
            dve.wait_ge(consts_made, 1)
            link(nc.vector.tensor_copy(len_f[:, :], len_i[:, :]))
            for c in range(C):
                last = nc.vector.tensor_scalar(mask_t[:, c, :], len_f[:, :], time_col[:, c:c + 1], None,
                                               ALU.is_gt, ALU.bypass)
            last.then_inc(mask_ready, 1)
            kernel_rows(0, 0, 0, True)
            angles(1, 1, True)
            angles(2, 0, False)
            kernel_rows(1, 1, 0, True)
            angles(3, 1, False)
            dve.wait_ge(mask_ready, 1)
            kernel_rows(2, 0, 1, False)
            outputs(0, 0, True)
            angles(4, 0, False)
            kernel_rows(3, 1, 1, False)
            outputs(1, 1, True)
            router(0)
            angles(5, 1, False)
            with dve.Fori(1, (G - 4) // 2) as i:
                for p in range(2):
                    kernel_rows(2 * i + 2 + p, p, i + 1, False)
                    outputs(2 * i + p, p, False)
                    router(2 * i + p - 1)
                    angles(2 * i + 4 + p, p, False)
            for g in range(G - 4, G):
                if g + 2 < G:
                    kernel_rows(g + 2, g % 2, (g + 2) // 2, False)
                if g == G - 1:
                    dve.wait_ge(log_read, G - 2)
                    choose(0, G - 2)
                outputs(g, g % 2, False)
                router(g - 1)
            router(G - 1)

            dve.wait_ge(log_read, G)
            choose(G - 2, G)
            dve.wait_ge(starts_marked, 1)
            dve.wait_ge(counted, 1)
            link(nc.vector.tensor_tensor_scan(run[:, :, :].rearrange("p e g -> p (e g)"),
                                              not_first[:, :, :].rearrange("p e g -> p (e g)"),
                                              conv_ps[:, 1, 0:E * G], 0.0, ALU.mult, ALU.add))
            ts(tiles[:, :], run[:, :, G - 1], 1.0 / P, HALF_DOWN, ALU.mult, ALU.add)
            ts(tiles[:, :], tiles[:, :], ROUND, ROUND, ALU.add, ALU.subtract)
            ts(tiles[:, :], tiles[:, :], 1.0, None, ALU.max, ALU.bypass)
            link(nc.vector.tensor_tensor_scan(ends[:, :], ones[:, 0:E], tiles[:, :], 0.0, ALU.mult, ALU.add))
            nc.vector.tensor_copy(ends_i[:, :], ends[:, :]).then_inc(ends_made, 1)
            tt(starts[:, :], ends[:, :], tiles[:, :], ALU.subtract)
            dve.wait_ge(spread_exp, 1)
            link(nc.vector.reduce_sum(total[:, :], spread[:, :, :], AX.X))
            link(nc.vector.reciprocal(total[:, :], total[:, :]))
            tt(weight[:, :, :], top2[:, :, :], total[:, :].unsqueeze(1).to_broadcast([P, K, G]), ALU.mult)
            tt(norm[:, :], weight[:, 0, :], weight[:, 1, :], ALU.add)
            link(nc.vector.reciprocal(norm[:, :], norm[:, :]))
            tt(weight[:, :, :], weight[:, :, :], norm[:, :].unsqueeze(1).to_broadcast([P, K, G]), ALU.mult)
            tt(dest[:, :, :], run[:, :, :], later_ps, ALU.add)
            link(nc.vector.scalar_tensor_tensor(dest[:, :, :], starts[:, :].unsqueeze(2).to_broadcast([P, E, G]),
                                                float(P), dest[:, :, :], ALU.mult, ALU.add))
            for k in range(K):
                tt(chosen[:, k, :, :], chosen[:, k, :, :], dest[:, :, :].rearrange("p e g -> p g e"), ALU.mult)
            link(nc.vector.reduce_sum(slot[:, :], chosen[:, :, :, :].rearrange("p k g e -> p (k g) e"), AX.X))
            ts(slot_q[:, :], slot[:, :], 1.0 / P, -HALF_DOWN, ALU.mult, ALU.add)
            ts(slot_q[:, :], slot_q[:, :], ROUND, ROUND, ALU.add, ALU.subtract)
            stt(slot[:, :], slot_q[:, :], -float(P), slot[:, :], ALU.mult, ALU.add)
            for q, (lo, hi) in enumerate(PIECES):
                js = slice(lo, hi)
                col = [P, hi - lo, MC]
                nc.vector.tensor_tensor(slot_hot[:, js, :], slot_q[:, js].unsqueeze(2).to_broadcast(col),
                                        iota_row[:, 0:MC].unsqueeze(1).to_broadcast(col),
                                        ALU.is_equal).then_inc(hot_made, 1)
                nc.vector.tensor_tensor(slot_row[:, js, :], slot[:, js].unsqueeze(2).to_broadcast([P, hi - lo, P]),
                                        iota_row[:, :].unsqueeze(1).to_broadcast([P, hi - lo, P]),
                                        ALU.is_equal).then_inc(hot_row_made, 1)
            dve.wait_ge(table_made, 1)
            ts(shift[:, :], table_ps[:, 0:MC], 0.0, float(NONE), ALU.is_equal, ALU.mult)
            stt(named[:, :], table_ps[:, 0:MC], -1.0, shift[:, :], ALU.add, ALU.add)
            nc.vector.tensor_copy(from_row[:, :], named[:, :]).then_inc(sources_made, 1)
            dve.wait_ge(sources_made, 1)
            ts(shift[:, :], table_ps[:, 0:MC], 0.0, spare[:, 0:1], ALU.is_equal, ALU.mult)
            stt(named[:, :], table_ps[:, 0:MC], -1.0, shift[:, :], ALU.add, ALU.add)
            link(nc.vector.tensor_copy(slot_weight[:, :], table_ps[:, MC:]))
            nc.vector.tensor_copy(to_row[:, :], named[:, :]).then_inc(lists_made, 1)
            tt(passed[:, :, :], iota_row[:, 0:MC].unsqueeze(2).to_broadcast([P, MC, E]),
               ends[:, :].unsqueeze(1).to_broadcast([P, MC, E]), ALU.is_ge)
            link(nc.vector.reduce_sum(tile_e[:, :], passed[:, :, :], AX.X))
            ts(tile_e[:, :], tile_e[:, :], float(E - 1), None, ALU.min, ALU.bypass)
            ts(tile_f[:, 1, :], tile_e[:, :], 1.0, None, ALU.add, ALU.bypass)
            ts(tile_f[:, 0, :], tile_e[:, :], 1.0 / WB, -(WB - 1) / (2.0 * WB), ALU.mult, ALU.add)
            ts(tile_f[:, 0, :], tile_f[:, 0, :], ROUND, ROUND, ALU.add, ALU.subtract)
            stt(tile_f[:, 0, :], tile_f[:, 0, :], -float(WB), tile_e[:, :], ALU.mult, ALU.add)
            nc.vector.tensor_copy(tile_i[:, :, :], tile_f[:, :, :]).then_inc(experts_made, 1)

            def turn_rest(t, p, first):
                dve.wait_ge(turned, t + 1)
                if not first:
                    dve.wait_ge(gu_done, t - 1)
                nc.vector.tensor_copy(ys_t[:, p, C // 2:, :], ytr_ps[:, L // 2:].rearrange("p (c n) -> p c n", n=P)
                                      ).then_inc(yst_dve, 1)

            def hidden(t, p, first):
                dve.wait_ge(silu_made, t + 1)
                if not first:
                    dve.wait_ge(hid_turned, t - 1)
                nc.vector.tensor_tensor(hid[:, p, :], silu[:, p, :], gu_ps[:, INTER:], ALU.mult).then_inc(hid_made, 1)

            def hidden_turned(t, p, first):
                dve.wait_ge(hid_turned, t + 1)
                if not first:
                    dve.wait_ge(down_done, t - 1)
                nc.vector.tensor_copy(hid_t[:, p, :], hid_ps).then_inc(hid_read, 1)

            def weight_of(t, p, first):
                if not first:
                    dve.wait_ge(od_act, t - 1)
                    dve.wait_ge(od_dve, t - 1)
                nc.vector.tensor_copy(weight_now[:, p:p + 1], slot_weight[:, bass.ds(t, 1)]).then_inc(weight_copied, 1)

            def weigh_rest(t, p, i, first):
                dve.wait_ge(down_done, t + 1)
                dve.wait_ge(weight_copied, t + 1)
                if not first:
                    dve.wait_ge(scattered[p], 16 * i)
                nc.vector.tensor_scalar(od[:, p, L // 2:], down_ps[:, 1, :], weight_now[:, p:p + 1], None,
                                        ALU.mult, ALU.bypass).then_inc(od_dve, 1)

            turn_rest(0, 0, True)
            weight_of(0, 0, True)
            hidden(0, 0, True)
            turn_rest(1, 1, True)
            hidden_turned(0, 0, True)
            weight_of(1, 1, True)
            hidden(1, 1, True)
            turn_rest(2, 0, False)
            weigh_rest(0, 0, 0, True)
            hidden_turned(1, 1, True)
            weight_of(2, 0, False)
            hidden(2, 0, False)
            turn_rest(3, 1, False)
            weigh_rest(1, 1, 0, True)
            hidden_turned(2, 0, False)

            def pair(i):
                for p in (1, 0):
                    weight_of(2 * i + 2 - p, p, False)
                    hidden(2 * i + 2 - p, p, False)
                    turn_rest(2 * i + 3 - p, 1 - p, False)
                    weigh_rest(2 * i + 1 - p, 1 - p, i, False)
                    hidden_turned(2 * i + 2 - p, p, False)

            used = tiles_in_use(dve)
            pairs(dve, used, pair)
            with dve.If(used >= MT - 2):
                for t in range(MT - 2, MT):
                    weight_of(t, t % 2, False)
                    hidden(t, t % 2, False)
                    if t + 1 < MT:
                        turn_rest(t + 1, (t + 1) % 2, False)
                    weigh_rest(t - 1, (t - 1) % 2, (t - 1) // 2, False)
                    hidden_turned(t, t % 2, False)
                weigh_rest(MT - 1, (MT - 1) % 2, (MT - 1) // 2, False)

        @block.tensor
        def _(pe):
            def products(g, p, first):
                pe.wait_ge(factors_made, g + 1)
                if not first:
                    pe.wait_ge(k_copied, g)
                for h in range(HG):
                    last = nc.tensor.matmul(k_ps[:, h, :], am[:, p, h, :], bm[:, p, h, :], start=True, stop=True)
                last.then_inc(k_made, 1)

            def convolve_channel(g, h, p, first):
                if not first:
                    pe.wait_ge(conv_read, g * HG + h - HG + 1)
                for d in range(C):
                    last = nc.tensor.matmul(conv_ps[:, h, d * B:C * B], toep[:, p, h, d * P:(d + 1) * P],
                                            u_t[:, p, h, 0:(C - d) * B], start=(d == 0), stop=(d == C - 1))
                last.then_inc(conv_done, 1)

            def convolve_first(g, between):
                pe.wait_ge(u_in[g], 16)
                for h in range(HG):
                    pe.wait_ge(toep_first[g][h], 16)
                    convolve_channel(g, h, g, g == 0)
                    if h == 0:
                        between()

            def convolve(g, p, i):
                pe.wait_ge(u_in[p], 16 * (i + 1))
                pe.wait_ge(toep_in[p], 16 * i)
                for h in range(HG):
                    convolve_channel(g, h, p, False)

            def stay_awake(n):
                for _ in range(n):
                    nc.tensor.matmul(log_ps[:, :], ones[:, :], ones[:, :], start=True, stop=True)

            def post(g, p, first):
                pe.wait_ge(conv_read, g * HG + HG)
                if not first:
                    pe.wait_ge(log_read, g)
                for c in range(C):
                    last = nc.tensor.matmul(log_ps[:, 0:E], y_t[:, p, c, :], gate_sb[:, c, :],
                                            start=(c == 0), stop=(c == C - 1))
                last.then_inc(log_done, 1)
                if not first:
                    pe.wait_ge(ytr_read, g)
                for c in range(C):
                    last = nc.tensor.transpose(ytr_ps[:, c * P:(c + 1) * P], y_t[:, p, c, :], ident[:, :])
                last.then_inc(post_done, 1)

            pe.wait_ge(gate_in, 16)
            pe.wait_ge(consts_made, 1)
            pe.wait_ge(coef_made, 1)
            stay_awake(4)
            products(0, 0, True)
            stay_awake(21)
            convolve_first(0, lambda: products(1, 1, False))
            for g in range(2, 4):
                products(g, g % 2, False)
            convolve_first(1, lambda: None)
            post(0, 0, True)
            products(4, 0, False)
            with pe.Fori(1, (G - 4) // 2) as i:
                for p in range(2):
                    convolve(2 * i + p, p, i)
                    post(2 * i + p - 1, 1 - p, False)
                    products(2 * i + 3 + p, 1 - p, False)
            for g in range(G - 4, G):
                convolve(g, g % 2, g // 2)
                post(g - 1, (g - 1) % 2, False)
                if g + 3 < G:
                    products(g + 3, (g + 3) % 2, False)
            post(G - 1, (G - 1) % 2, False)

            pe.wait_ge(log_read, G)
            stay_awake(8)
            pe.wait_ge(chosen_made, 2)
            nc.tensor.matmul(later_ps, not_before[:, :], both[:, :, :], start=True, stop=True)
            nc.tensor.matmul(count_ps, ones[:, :], both[:, :, :], start=True, stop=True).then_inc(counted, 1)
            pe.wait_ge(ends_made, 1)
            stay_awake(16)
            for q, (lo, hi) in enumerate(PIECES):
                pe.wait_ge(hot_row_made, q + 1)
                pe.wait_ge(hot_weight_made, q + 1)
                pe.wait_ge(hot_token_made, q + 1)
                for j in range(lo, hi):
                    last = nc.tensor.matmul(table_ps, slot_row[:, j, :], slot_tile[:, j, :],
                                            start=(j == 0), stop=(j == K * G - 1))
            last.then_inc(table_made, 1)
            stay_awake(20)

            def gate_up(t, p):
                buf = pe.value_load(tile_i[0:1, 0, bass.ds(t, 1)], min_val=0, max_val=WB - 1)
                need = pe.value_load(tile_i[0:1, 1, bass.ds(t, 1)], min_val=1, max_val=E)
                pe.wait_ge(weights_ready, need)
                pe.wait_ge(yst_act, t + 1)
                pe.wait_ge(yst_dve, t + 1)
                for c in range(C):
                    last = nc.tensor.matmul(gu_ps, ys_t[:, p, c, :], w_gu[:, bass.ds(buf * (C * GU) + c * GU, GU)],
                                            start=(c == 0), stop=(c == C - 1))
                last.then_inc(gu_done, 1)

            def turn(t, p, i):
                pe.wait_ge(gathered[p], 16 * (i + 1))
                for c in range(C):
                    last = nc.tensor.transpose(ytr_ps[:, c * P:(c + 1) * P], ys[:, p, c * P:(c + 1) * P], ident[:, :])
                last.then_inc(turned, 1)

            def down(t, p, first):
                buf = pe.value_load(tile_i[0:1, 0, bass.ds(t, 1)], min_val=0, max_val=WB - 1)
                pe.wait_ge(hid_read, t + 1)
                if not first:
                    pe.wait_ge(od_act, t)
                    pe.wait_ge(od_dve, t)
                for n in range(2):
                    last = nc.tensor.matmul(down_ps[:, n, :], hid_t[:, p, :],
                                            w_d[:, bass.ds(buf * L + n * (L // 2), L // 2)], start=True, stop=True)
                last.then_inc(down_done, 1)

            def turn_hidden(t, p):
                pe.wait_ge(hid_made, t + 1)
                nc.tensor.transpose(hid_ps, hid[:, p, :], ident[:, :]).then_inc(hid_turned, 1)

            turn(0, 0, 0)
            pe.wait_ge(experts_made, 1)
            gate_up(0, 0)
            turn(1, 1, 0)
            turn_hidden(0, 0)
            gate_up(1, 1)
            turn(2, 0, 1)
            down(0, 0, True)
            turn_hidden(1, 1)
            gate_up(2, 0)
            turn(3, 1, 1)
            down(1, 1, False)
            turn_hidden(2, 0)

            def pair(i):
                for p in (1, 0):
                    gate_up(2 * i + 2 - p, p)
                    turn(2 * i + 3 - p, 1 - p, i + 1)
                    down(2 * i + 1 - p, 1 - p, False)
                    turn_hidden(2 * i + 2 - p, p)

            used = tiles_in_use(pe)
            pairs(pe, used, pair)
            with pe.If(used >= MT - 2):
                for t in range(MT - 2, MT):
                    gate_up(t, t % 2)
                    if t + 1 < MT:
                        turn(t + 1, (t + 1) % 2, (t + 1) // 2)
                    down(t - 1, (t - 1) % 2, False)
                    turn_hidden(t, t % 2)
                down(MT - 1, (MT - 1) % 2, False)


def kernel(x, itok_B_8_3872, L0_cond_log_dt, L0_cond_C, L0_cond_log_A_real, L0_cond_A_imag, L0_cond_D,
           L0_ffn_gate_w, L0_ffn_u, L0_ffn_g, L0_ffn_d):
    import numpy as np
    import concourse.bacc as bacc
    from concourse.bass_utils import run_bass_kernel_spmd

    x = np.asarray(x)
    c = np.asarray(L0_cond_C)
    gu = np.stack([np.asarray(L0_ffn_g), np.asarray(L0_ffn_u)]).reshape(2, E, INTER, C, P)
    arrays = {
        "x_time": x.reshape(B, H, C, P)[:, :, :, ::-1].transpose(3, 1, 2, 0).reshape(P, H, C * B),
        "x_rows": x.transpose(1, 0, 2).reshape(TOK, L),
        "lengths": np.asarray(itok_B_8_3872),
        "params": np.tile(np.stack([np.broadcast_to(np.asarray(L0_cond_log_dt), (N, H)),
                                    np.asarray(L0_cond_log_A_real).T, np.asarray(L0_cond_A_imag).T,
                                    c[:, :, 0].T, c[:, :, 1].T], axis=1), (2, 1, 1)),
        "skip": np.asarray(L0_cond_D).reshape(1, H),
        "gate_t": np.asarray(L0_ffn_gate_w).reshape(E, C, P).transpose(2, 1, 0),
        "gu_t": gu.transpose(1, 4, 3, 0, 2).reshape(E, P, C * 2 * INTER),
        "d_t": np.asarray(L0_ffn_d).reshape(L, E, INTER).transpose(1, 2, 0),
    }
    arrays = {name: np.ascontiguousarray(a) for name, a in arrays.items()}
    nc = bacc.Bacc("TRN2", target_bir_lowering=False, num_devices=1)
    ins = [nc.dram_tensor(name, a.shape, mybir.dt.from_np(a.dtype), kind="ExternalInput").ap()
           for name, a in arrays.items()]
    out = nc.dram_tensor("out", (TOK + P, L), mybir.dt.float32, kind="ExternalOutput").ap()
    build(nc, *ins, out)
    got = run_bass_kernel_spmd(nc, [arrays], core_ids=[0]).results[0]["out"]
    return np.ascontiguousarray(got[:TOK].reshape(H, B, L).transpose(1, 0, 2))
```

```python
import math
from contextlib import ExitStack

import concourse.bass as bass
from concourse import mybir

B, H, L = 32, 64, 1024
N = 64
P = 128
E, INTER, K = 16, 112, 2
TOK = B * H
C = L // P
HG = P // B
G = H // HG
LO = 32
SEG = 3 * LO
KROW = L + P
MT = -(-K * TOK // P) + E - 1
LEAST = K * TOK // P

LOG2E = 1.0 / math.log(2.0)
LN2_HI = 0.693359375
LN2_LO = math.log(2.0) - LN2_HI
TWO_PI = 2.0 * math.pi
TWO_PI_HI = 6.28125
TWO_PI_MID = round((TWO_PI - TWO_PI_HI) * 2**20) / 2**20
TWO_PI_LO = TWO_PI - TWO_PI_HI - TWO_PI_MID
ROUND = 1.5 * 2.0**23
PI_IN = 3.1415925
EXP_TERMS = 7
GU = 2 * INTER
IG = P + E
IGS = 512 // IG
MC = MT + 1
WB = 4
PIECES = ((0, 4), (4, 8), (8, 16), (16, 24), (24, K * G))
NONE = 4 * K * TOK
HALF_DOWN = (P - 1) / (2.0 * P)


def build(nc, x_time, x_rows, lengths, params, skip, gate_t, gu_t, d_t, out):
    fp32, i32, u32 = mybir.dt.float32, mybir.dt.int32, mybir.dt.uint32
    ALU, ACT, AX = mybir.AluOpType, mybir.ActivationFunctionType, mybir.AxisListType

    ctx = ExitStack()
    with ctx:
        def sb(name, shape, dt=fp32):
            return ctx.enter_context(nc.sbuf_tensor(name, shape, dt))

        def pb(name, shape, dt=fp32):
            return ctx.enter_context(nc.psum_tensor(name, shape, dt))

        def sem(name):
            return ctx.enter_context(nc.semaphore(name))

        k_rows = nc.dram_tensor("k_rows", [H, KROW], fp32)
        y_rows = nc.dram_tensor("y_rows", [TOK, L], fp32).ap()

        flat = sb("arena", [P, 2 * HG * L + H * 2 * LO + 2 * HG * C * B + 2 * C * P])
        toep = flat[:, 0:2 * HG * L].rearrange("p (s h l) -> p s h l", s=2, h=HG)
        at = 2 * HG * L
        mag = flat[:, at:at + H * 2 * LO].rearrange("p (h l) -> p h l", h=H)
        at += H * 2 * LO
        u_t = flat[:, at:at + 2 * HG * C * B].rearrange("p (s h n) -> p s h n", s=2, h=HG)
        at += 2 * HG * C * B
        y_t = flat[:, at:at + 2 * C * P].rearrange("p (s c n) -> p s c n", s=2, c=C)
        slot_row = flat[:, 0:K * G * P].rearrange("p (j r) -> p j r", j=K * G)
        slot_hot = flat[:, K * G * (P + 2 * MC):K * G * (P + 3 * MC)].rearrange("p (j n) -> p j n", j=K * G)
        slot_tile = flat[:, K * G * P:K * G * (P + 2 * MC)].rearrange("p (j n) -> p j n", j=K * G)
        par = sb("par", [P, 5, H])
        LOGDT, LOGA, AIM, CRE, CIM = range(5)
        skip_row = sb("skip_row", [1, H])
        tmp = sb("tmp", [P, 24, H])
        tmp_i = sb("tmp_i", [P, 2, H], i32)
        decay = sb("decay", [P, H])
        omega = sb("omega", [P, H])
        cs_re = sb("cs_re", [P, H])
        cs_im = sb("cs_im", [P, H])
        steps = sb("steps", [P, SEG])
        off_turns = sb("off_turns", [P, SEG])
        off_rad = sb("off_rad", [P, SEG])
        phase = sb("phase", [P, 2, HG, SEG])
        turns = sb("turns", [P, 2, HG, SEG])
        angle = sb("angle", [P, 2, HG, SEG])
        wave = sb("wave", [P, 2, HG, SEG])
        am = sb("am", [P, 2, HG, LO])
        am2 = sb("am2", [P, 2, HG, LO])
        bm = sb("bm", [P, 2, HG, LO])
        k_sb = sb("k_sb", [LO, 2, HG, LO])
        zero = sb("zero", [H, P])
        y_tok = sb("y_tok", [P, 2, C, IG])
        mask_t = sb("mask_t", [P, C, B])
        len_i = sb("len_i", [P, B], i32)
        len_f = sb("len_f", [P, B])
        time_col = sb("time_col", [P, C])
        ident = sb("ident", [P, P])
        ident_gate = sb("ident_gate", [P, C, IG])
        logits = sb("logits", [P, G, E])
        top_v = sb("top_v", [P, G, 8])
        top_i = sb("top_i", [P, G, 8], u32)

        iota_row = sb("iota_row", [P, P])
        not_before = sb("not_before", [P, P])
        ones = sb("ones", [P, P])
        token_no = sb("token_no", [P, K * G])
        spread = sb("spread", [P, G, E])
        total = sb("total", [P, G])
        top2 = sb("top2", [P, K, G])
        weight = sb("weight", [P, K, G])
        norm = sb("norm", [P, G])
        expert = sb("expert", [P, K, G])
        chosen = sb("chosen", [P, K, G, E])
        both = sb("both", [P, E, G])
        not_first = sb("not_first", [P, E, G])
        run = sb("run", [P, E, G])
        tiles = sb("tiles", [P, E])
        ends = sb("ends", [P, E])
        starts = sb("starts", [P, E])
        dest = sb("dest", [P, E, G])
        slot = sb("slot", [P, K * G])
        slot_q = sb("slot_q", [P, K * G])
        named = sb("named", [P, MC])
        shift = sb("shift", [P, MC])
        slot_weight = sb("slot_weight", [P, MC])
        spare = sb("spare", [P, 1])
        from_row = sb("from_row", [P, MC], i32)
        to_row = sb("to_row", [P, MC], i32)
        passed = sb("passed", [P, MC, E])
        tile_e = sb("tile_e", [P, MC])
        tile_f = sb("tile_f", [P, 2, MC])
        tile_i = sb("tile_i", [P, 2, MC], i32)
        ends_i = sb("ends_i", [P, E], i32)

        w_gu = sb("w_gu", [P, WB * C * GU])
        w_d = sb("w_d", [INTER, WB * L])
        ys = sb("ys", [P, 2, L])
        ys_t = sb("ys_t", [P, 2, C, P])
        weight_now = sb("weight_now", [P, 2])
        silu = sb("silu", [P, 2, INTER])
        hid = sb("hid", [P, 2, INTER])
        hid_t = sb("hid_t", [INTER, 2, P])
        od = sb("od", [P, 2, L])

        conv_ps = pb("conv_ps", [P, HG, 512])
        k_bank = pb("k_bank", [P, HG, LO])
        k_ps = k_bank[0:LO, :, :]
        later_ps = conv_ps[:, 0, 0:E * G].rearrange("p (e g) -> p e g", e=E)
        count_ps = conv_ps[:, 1, 0:E * G].rearrange("p (e g) -> p e g", e=E)
        table_ps = conv_ps[:, 2, 0:2 * MC]
        down_ps = conv_ps[:, 0:2, :]
        gu_ps = conv_ps[:, 2, 0:GU]
        hid_ps = conv_ps[0:INTER, 3, 0:P]
        turn_ps = pb("turn_ps", [P, -(-C // IGS), 512])
        ytr_ps = turn_ps[:, 0:2, :].rearrange("p b n -> p (b n)")

        par_in = sem("par_in")
        len_in = sem("len_in")
        gate_in = sem("gate_in")
        ys_cleared = sem("ys_cleared")
        x_copied = sem("x_copied")
        spare_out = sem("spare_out")
        zero_made = sem("zero_made")
        pads_out = sem("pads_out")
        chain = sem("chain")
        pool_chain = sem("pool_chain")
        half_sin = sem("half_sin")
        trig_in = sem("trig_in")
        decay_made = sem("decay_made")
        omega_made = sem("omega_made")
        square_made = sem("square_made")
        coef_made = sem("coef_made")
        consts_made = sem("consts_made")
        mask_ready = sem("mask_ready")
        growth_made = sem("growth_made")
        mag_made = sem("mag_made")
        phase_made = sem("phase_made")
        angle_steps = sem("angle_steps")
        angle_made = sem("angle_made")
        wave_made = sem("wave_made")
        am_steps = sem("am_steps")
        factors_made = sem("factors_made")
        k_made = sem("k_made")
        k_copied = sem("k_copied")
        k_added = sem("k_added")
        k_stored = [sem(f"k_stored{i}") for i in range(2)]
        toep_in = [sem(f"toep_in{i}") for i in range(2)]
        toep_first = [[sem(f"toep_first{p}_{h}") for h in range(HG)] for p in range(2)]
        u_in = [sem(f"u_in{i}") for i in range(2)]
        conv_done = sem("conv_done")
        conv_read = sem("conv_read")
        log_made = sem("log_made")
        post_done = sem("post_done")
        ytr_read = sem("ytr_read")
        top_made = sem("top_made")
        y_stored = [sem(f"y_stored{i}") for i in range(2)]

        starts_marked = sem("starts_marked")
        ident_copied = sem("ident_copied")
        top_found = sem("top_found")
        spread_made = sem("spread_made")
        spread_exp = sem("spread_exp")
        chosen_made = sem("chosen_made")
        counted = sem("counted")
        hot_made = sem("hot_made")
        hot_row_made = sem("hot_row_made")
        hot_weight_made = sem("hot_weight_made")
        hot_token_made = sem("hot_token_made")
        sources_made = sem("sources_made")
        table_made = sem("table_made")
        lists_made = sem("lists_made")
        experts_made = sem("experts_made")
        ends_made = sem("ends_made")
        weights_ready = sem("weights_ready")
        gu_done = sem("gu_done")
        yst_act = sem("yst_act")
        yst_dve = sem("yst_dve")
        silu_made = sem("silu_made")
        hid_made = sem("hid_made")
        turned = sem("turned")
        hid_turned = sem("hid_turned")
        hid_read = sem("hid_read")
        down_done = sem("down_done")
        od_act = sem("od_act")
        od_dve = sem("od_dve")
        weight_copied = sem("weight_copied")
        w_in = [sem(f"w_in{i}") for i in range(WB)]
        gathered = [sem(f"gathered{i}") for i in range(2)]
        scattered = [sem(f"scattered{i}") for i in range(2)]

        block = ctx.enter_context(nc.Block())

        def tiles_in_use(eng):
            return eng.value_load(ends_i[0:1, E - 1:E], min_val=LEAST, max_val=MT)

        def pairs(eng, used, pair):
            pair(1)
            with eng.Fori(1, (LEAST - 1) // 4 + 1) as i:
                pair(2 * i)
                pair(2 * i + 1)
            with eng.Fori((LEAST - 1) // 2 + 1, (MT - 3) // 2) as i:
                with eng.If(used >= 2 * i + 1):
                    pair(i)

        def first_step(s):
            return min(s - (s + 1) % 2, MT - 2)

        def hs(g):
            return bass.ds(g * HG, HG)

        @block.sync
        def _(sp):
            sp.dma_start(par[:, :, :], params).then_inc(par_in, 16)
            sp.dma_start(skip_row[:, :], skip).then_inc(par_in, 16)
            sp.dma_start(len_i[:, :], lengths.partition_broadcast(P)).then_inc(len_in, 16)
            sp.dma_start(ident_gate[:, :, P:], gate_t).then_inc(gate_in, 16)

            def copy_x(q):
                part = slice(q * (TOK // 8), (q + 1) * (TOK // 8))
                sp.dma_start(out[part, :], x_rows[part, :]).then_inc(x_copied, 16)

            sp.wait_ge(ys_cleared, 1)
            sp.dma_start(out[TOK:, :], ys[:, 0, :]).then_inc(spare_out, 16)
            sp.wait_ge(zero_made, 1)
            sp.dma_start(k_rows.ap()[:, 0:P - 1], zero[:, 0:P - 1]).then_inc(pads_out, 16)
            for q in range(6):
                copy_x(q)
            sp.wait_ge(pads_out, 16)

            def load_expert(e):
                s = e % WB
                sp.dma_start(w_gu[:, s * C * GU:(s + 1) * C * GU], gu_t[e]).then_inc(w_in[s], 16)
                sp.dma_start(w_d[:, s * L:(s + 1) * L], d_t[e]).then_inc(w_in[s], 16)

            for g in range(G):
                p, i = g % 2, g // 2
                sp.wait_ge(k_added, g + 1)
                sp.dma_start(bass.AP(k_rows, g * HG * KROW + P - 1, [[LO, LO], [KROW, HG], [1, LO]]),
                             k_sb[:, p, :, :]).then_inc(k_stored[p], 16)
                if g >= 2:
                    sp.wait_ge(conv_done, (g - 1) * HG)
                sp.dma_start(u_t[:, p, :, :], x_time[:, g * HG:(g + 1) * HG, :]).then_inc(u_in[p], 16)
                sp.wait_ge(k_stored[p], 16 * (i + 1))
                if g < 2:
                    for h in range(HG):
                        sp.dma_start(toep[:, p, h, :], bass.AP(k_rows, (g * HG + h) * KROW, [[1, P], [1, L]])
                                     ).then_inc(toep_first[p][h], 16)
                else:
                    sp.dma_start(toep[:, p, :, :], bass.AP(k_rows, g * HG * KROW, [[1, P], [KROW, HG], [1, L]])
                                 ).then_inc(toep_in[p], 16)
                if g in (3, 5, 7, 9):
                    load_expert((g - 3) // 2)
                if g in (11, 13):
                    copy_x(6 + (g - 11) // 2)
            for e in range(WB):
                sp.wait_ge(w_in[e % WB], 32)
                sp.sem_inc(weights_ready, 1)
            sp.wait_ge(ends_made, 1)
            sp.wait_ge(lists_made, 1)
            for e in range(WB, E):
                end = sp.value_load(ends_i[0:1, e - WB:e - WB + 1], min_val=1, max_val=MT)
                sp.wait_ge(down_done, end)
                load_expert(e)
                sp.wait_ge(w_in[e % WB], 32 * (e // WB + 1))
                sp.sem_inc(weights_ready, 1)

        @block.gpsimd
        def _(pool):
            made = [0]

            def link(ins):
                made[0] += 1
                ins.then_inc(pool_chain, 1)
                pool.wait_ge(pool_chain, made[0])

            nc.gpsimd.memset(zero[:, :], 0.0).then_inc(zero_made, 1)
            for k, m in ((0, LO), (1, LO), (2, 1)):
                nc.gpsimd.iota(steps[:, k * LO:(k + 1) * LO], [[m, LO]], base=0, channel_multiplier=0,
                               allow_small_or_imprecise_dtypes=True)
            nc.gpsimd.iota(time_col[:, :], [[P, C]], base=0, channel_multiplier=1,
                           allow_small_or_imprecise_dtypes=True)
            nc.gpsimd.iota(iota_row[:, :], [[1, P]], base=0, channel_multiplier=0,
                           allow_small_or_imprecise_dtypes=True)
            nc.gpsimd.iota(token_no[:, :], [[0, K], [P, G]], base=1, channel_multiplier=1,
                           allow_small_or_imprecise_dtypes=True)
            nc.gpsimd.iota(spare[:, :], [[0, 1]], base=TOK + 1, channel_multiplier=1,
                           allow_small_or_imprecise_dtypes=True)
            nc.gpsimd.memset(ys[:, :, :], 0.0).then_inc(ys_cleared, 1)
            nc.gpsimd.memset(ones[:, :], 1.0)
            link(nc.gpsimd.memset(not_before[:, :], 0.0))
            nc.gpsimd.affine_select(out=not_before[:, :], in_=not_before[:, :], compare_op=ALU.is_gt, fill=-1.0,
                                    base=0, pattern=[[1, P]], channel_multiplier=-1)
            link(nc.gpsimd.memset(ident[:, :], 0.0))
            nc.gpsimd.affine_select(out=ident[:, :], in_=ident[:, :], compare_op=ALU.not_equal, fill=1.0,
                                    base=0, pattern=[[-1, P]], channel_multiplier=1).then_inc(consts_made, 1)
            pool.wait_ge(consts_made, 1)

            def growth(lo, hi):
                nc.gpsimd.tensor_tensor(mag[:, lo:hi, :],
                                        decay[:, lo:hi].unsqueeze(2).to_broadcast([P, hi - lo, 2 * LO]),
                                        steps[:, LO:].unsqueeze(1).to_broadcast([P, hi - lo, 2 * LO]),
                                        ALU.mult).then_inc(growth_made, 1)

            def phases(g, p, first):
                if not first:
                    pool.wait_ge(angle_made, g - 1)
                nc.gpsimd.tensor_tensor(phase[:, p, :, :],
                                        omega[:, hs(g)].unsqueeze(2).to_broadcast([P, HG, SEG]),
                                        steps[:, :].unsqueeze(1).to_broadcast([P, HG, SEG]),
                                        ALU.mult).then_inc(phase_made, 1)

            def factors(g, p, first):
                pool.wait_ge(wave_made, g + 1)
                if not first:
                    pool.wait_ge(k_made, g - 1)
                bc = [P, HG, LO]
                nc.gpsimd.tensor_tensor(am[:, p, :, :], wave[:, p, :, 0:LO],
                                        cs_re[:, hs(g)].unsqueeze(2).to_broadcast(bc), ALU.mult).then_inc(am_steps, 1)
                nc.gpsimd.tensor_tensor(am2[:, p, :, :], wave[:, p, :, LO:2 * LO],
                                        cs_im[:, hs(g)].unsqueeze(2).to_broadcast(bc), ALU.mult).then_inc(am_steps, 1)
                nc.gpsimd.tensor_tensor(bm[:, p, :, :], wave[:, p, :, 2 * LO:], mag[:, hs(g), LO:],
                                        ALU.mult).then_inc(am_steps, 1)
                pool.wait_ge(am_steps, 4 * g + 3)
                nc.gpsimd.tensor_tensor(am[:, p, :, :], am[:, p, :, :], am2[:, p, :, :], ALU.add).then_inc(am_steps, 1)
                pool.wait_ge(am_steps, 4 * g + 4)
                nc.gpsimd.tensor_tensor(am[:, p, :, :], am[:, p, :, :], mag[:, hs(g), 0:LO],
                                        ALU.mult).then_inc(factors_made, 1)

            pool.wait_ge(omega_made, 1)
            phases(0, 0, True)
            pool.wait_ge(decay_made, 1)
            growth(0, 2 * HG)
            phases(1, 1, True)
            link(nc.gpsimd.tensor_tensor(tmp[:, 22, :], tmp[:, 5, :], tmp[:, 5, :], ALU.mult))
            link(nc.gpsimd.tensor_tensor(tmp[:, 23, :], par[:, AIM, :], par[:, AIM, :], ALU.mult))
            nc.gpsimd.tensor_tensor(tmp[:, 22, :], tmp[:, 22, :], tmp[:, 23, :], ALU.add).then_inc(square_made, 1)
            growth(2 * HG, H)
            pool.wait_ge(coef_made, 2)
            pool.wait_ge(mag_made, 1)
            for p in range(2):
                factors(p, p, True)
                phases(2 + p, p, False)
            nc.gpsimd.tensor_copy(ident_gate[:, :, 0:P], ident[:, :].unsqueeze(1).to_broadcast([P, C, P])
                                  ).then_inc(ident_copied, 1)
            link(nc.gpsimd.memset(not_first[:, :, :], 1.0))
            nc.gpsimd.memset(not_first[:, :, 0:1], 0.0).then_inc(starts_marked, 1)
            pool.wait_ge(mag_made, 2)
            with pool.Fori(1, G // 2 - 1) as i:
                for p in range(2):
                    factors(2 * i + p, p, False)
                    phases(2 * i + 2 + p, p, False)
            for p in range(2):
                factors(G - 2 + p, p, False)

            weights = weight[:, :, :].rearrange("p k g -> p (k g)")
            for q, (lo, hi) in enumerate(PIECES):
                js = slice(lo, hi)
                pool.wait_ge(hot_made, q + 1)
                nc.gpsimd.tensor_tensor(slot_tile[:, js, 0:MC], slot_hot[:, js, :],
                                        token_no[:, js].unsqueeze(2).to_broadcast([P, hi - lo, MC]),
                                        ALU.mult).then_inc(hot_token_made, 1)
                nc.gpsimd.tensor_tensor(slot_tile[:, js, MC:], slot_hot[:, js, :],
                                        weights[:, js].unsqueeze(2).to_broadcast([P, hi - lo, MC]),
                                        ALU.mult).then_inc(hot_weight_made, 1)

            def gather(t):
                if t >= 2:
                    pool.wait_ge(turned, t - 1)
                nc.gpsimd.indirect_dma_start(
                    out=ys[:, t % 2, :], out_offset=None, in_=y_rows,
                    in_offset=bass.IndirectOffsetOnAxis(ap=from_row[:, t:t + 1], axis=0),
                    bounds_check=TOK - 1, oob_is_err=False).then_inc(gathered[t % 2], 16)

            def scatter(t):
                pool.wait_ge(od_act, t + 1)
                pool.wait_ge(od_dve, t + 1)
                if t >= 1:
                    pool.wait_ge(scattered[(t - 1) % 2], 16 * ((t - 1) // 2 + 1))
                nc.gpsimd.indirect_dma_start(
                    out=out, out_offset=bass.IndirectOffsetOnAxis(ap=to_row[:, t:t + 1], axis=0),
                    in_=od[:, t % 2, :], in_offset=None, compute_op=ALU.add,
                    bounds_check=TOK + P - 1, oob_is_err=True).then_inc(scattered[t % 2], 16)

            pool.wait_ge(sources_made, 1)
            for p in range(2):
                pool.wait_ge(y_stored[p], 16 * (G // 2))
            gather(0)
            gather(1)
            gather(2)
            pool.wait_ge(lists_made, 1)
            pool.wait_ge(x_copied, 8 * 16)
            pool.wait_ge(spare_out, 16)
            used = tiles_in_use(pool)
            for t in range(1, MT + 2):
                if t + 2 < MT:
                    if first_step(t + 1) <= LEAST:
                        gather(t + 2)
                    else:
                        with pool.If(used >= first_step(t + 1)):
                            gather(t + 2)
                if t >= 2:
                    if first_step(t - 1) <= LEAST:
                        scatter(t - 2)
                    else:
                        with pool.If(used >= first_step(t - 1)):
                            scatter(t - 2)
            with pool.If(used >= MT - 2):
                pool.wait_ge(scattered[0], 16 * ((MT + 1) // 2))
                pool.wait_ge(scattered[1], 16 * (MT // 2))
            for p in range(2):
                pool.wait_ge(scattered[p], (used + 1) // 2 * 16)

        @block.scalar
        def _(act):
            act.wait_ge(growth_made, 1)
            nc.scalar.activation(mag[:, 0:2 * HG, :], mag[:, 0:2 * HG, :], ACT.Exp).then_inc(mag_made, 1)
            act.wait_ge(trig_in, 1)
            nc.scalar.activation(tmp[:, 10, :], tmp[:, 9, :], ACT.Sin, scale=0.5)
            nc.scalar.activation(tmp[:, 11, :], tmp[:, 9, :], ACT.Sin).then_inc(half_sin, 1)

            def waves(g, p, first):
                act.wait_ge(angle_made, g + 1)
                if not first:
                    act.wait_ge(factors_made, g - 1)
                nc.scalar.activation(wave[:, p, :, :], angle[:, p, :, :], ACT.Sin).then_inc(wave_made, 1)

            def rows_out(g, p, i, first):
                act.wait_ge(post_done, g + 1)
                if not first:
                    act.wait_ge(y_stored[p], 16 * i)
                    act.wait_ge(log_made, g - 1)
                full = C // IGS
                nc.scalar.copy(y_tok[:, p, 0:full * IGS, :].rearrange("p (b c) n -> p b (c n)", c=IGS),
                               turn_ps[:, 0:full, 0:IGS * IG]).then_inc(ytr_read, 1)
                nc.scalar.copy(y_tok[:, p, full * IGS:, :],
                               turn_ps[:, full, 0:(C - full * IGS) * IG].rearrange("p (c n) -> p c n", n=IG)
                               ).then_inc(ytr_read, 1)
                act.wait_ge(ytr_read, 2 * g + 2)
                act.dma_start(y_rows[bass.ds(g * P, P), :].rearrange("t (c n) -> t c n", n=P), y_tok[:, p, :, 0:P]
                              ).then_inc(y_stored[p], 16)

            for g in range(2):
                waves(g, g % 2, True)
            act.wait_ge(growth_made, 2)
            nc.scalar.activation(mag[:, 2 * HG:, :], mag[:, 2 * HG:, :], ACT.Exp).then_inc(mag_made, 1)
            for g in range(2, 5):
                waves(g, g % 2, False)
            for p in range(2):
                rows_out(p, p, 0, True)
                waves(5 + p, 1 - p, False)
            with act.Fori(1, (G - 6) // 2) as i:
                for p in range(2):
                    rows_out(2 * i + p, p, i, False)
                    waves(2 * i + 5 + p, 1 - p, False)
            for g in range(G - 6, G):
                rows_out(g, g % 2, g // 2, False)
                if g + 5 < G:
                    waves(g + 5, (g + 5) % 2, False)

            act.wait_ge(spread_made, 2)
            nc.scalar.activation(spread[:, :, :], spread[:, :, :], ACT.Exp)
            nc.scalar.activation(top2[:, :, :], top2[:, :, :], ACT.Exp).then_inc(spread_exp, 1)
            nc.scalar.activation(silu[:, 0, 0:1], len_f[:, 0:1], ACT.Silu)

            def turn_half(t, p, first):
                act.wait_ge(turned, t + 1)
                if not first:
                    act.wait_ge(gu_done, t - 1)
                nc.scalar.copy(ys_t[:, p, 0:C // 2, :], ytr_ps[:, 0:L // 2].rearrange("p (c n) -> p c n", n=P)
                               ).then_inc(yst_act, 1)

            def gate(t, p, first):
                act.wait_ge(gu_done, t + 1)
                if not first:
                    act.wait_ge(hid_made, t - 1)
                nc.scalar.activation(silu[:, p, :], gu_ps[:, 0:INTER], ACT.Silu).then_inc(silu_made, 1)

            def weigh_half(t, p, i, first):
                act.wait_ge(down_done, t + 1)
                act.wait_ge(weight_copied, t + 1)
                if not first:
                    act.wait_ge(scattered[p], 16 * i)
                nc.scalar.mul(od[:, p, 0:L // 2], down_ps[:, 0, :], weight_now[:, p:p + 1]).then_inc(od_act, 1)

            turn_half(0, 0, True)
            gate(0, 0, True)
            turn_half(1, 1, True)
            gate(1, 1, True)
            turn_half(2, 0, False)
            weigh_half(0, 0, 0, True)
            gate(2, 0, False)
            turn_half(3, 1, False)
            weigh_half(1, 1, 0, True)

            def pair(i):
                for p in (1, 0):
                    gate(2 * i + 2 - p, p, False)
                    turn_half(2 * i + 3 - p, 1 - p, False)
                    weigh_half(2 * i + 1 - p, 1 - p, i, False)

            act.wait_ge(ends_made, 1)
            used = tiles_in_use(act)
            pairs(act, used, pair)
            with act.If(used >= MT - 2):
                for t in range(MT - 2, MT):
                    gate(t, t % 2, False)
                    if t + 1 < MT:
                        turn_half(t + 1, (t + 1) % 2, False)
                    weigh_half(t - 1, (t - 1) % 2, (t - 1) // 2, False)
                weigh_half(MT - 1, (MT - 1) % 2, (MT - 1) // 2, False)

        @block.vector
        def _(dve):
            vec = nc.vector
            made = [0]

            def link(ins):
                made[0] += 1
                ins.then_inc(chain, 1)
                dve.wait_ge(chain, made[0])

            def links(*instructions):
                for ins in instructions:
                    ins.then_inc(chain, 1)
                made[0] += len(instructions)
                dve.wait_ge(chain, made[0])

            def tt(out, a, b, op):
                link(nc.vector.tensor_tensor(out, a, b, op))

            def ts(out, a, s1, s2, op0, op1):
                link(nc.vector.tensor_scalar(out, a, s1, s2, op0, op1))

            def stt(out, a, s, b, op0, op1):
                link(nc.vector.scalar_tensor_tensor(out, a, s, b, op0, op1))

            def t(i, n=1):
                return tmp[:, i, :] if n == 1 else tmp[:, i:i + n, :]

            for part, quarters in ((0, (1, 2, 1)), (1, (2, -1, 0))):
                for k, q in enumerate(quarters):
                    rows, cols = slice(part * N, part * N + N), slice(k * LO, (k + 1) * LO)
                    link(nc.vector.memset(off_turns[rows, cols], q * 0.25))
                    link(nc.vector.memset(off_rad[rows, cols], q * 0.25 * TWO_PI))
            dve.wait_ge(par_in, 32)
            logs = par[:, LOGDT:LOGA + 1, :]
            k2, r2, p2 = t(0, 2), t(2, 2), t(4, 2)
            ts(k2, logs, LOG2E, ROUND, ALU.mult, ALU.add)
            ts(k2, k2, ROUND, -126.0, ALU.subtract, ALU.max)
            stt(r2, k2, -LN2_HI, logs, ALU.mult, ALU.add)
            stt(r2, k2, -LN2_LO, r2, ALU.mult, ALU.add)
            ts(p2, r2, 1.0 / math.factorial(EXP_TERMS), None, ALU.mult, ALU.bypass)
            for n in range(EXP_TERMS - 1, 0, -1):
                stt(p2, p2, 1.0 / math.factorial(n), r2, ALU.add, ALU.mult)
            ts(tmp_i[:, :, :], k2, 127.0, 2.0**23, ALU.add, ALU.mult)
            stt(p2, p2, 1.0, tmp_i[:, :, :].bitcast(fp32), ALU.add, ALU.mult)
            dt, a_abs, a_imag = t(4), t(5), par[:, AIM, :]
            link(nc.vector.scalar_tensor_tensor(decay[:, :], a_abs, -1.0, dt, ALU.mult, ALU.mult))
            nc.vector.tensor_tensor(omega[:, :], a_imag, dt, ALU.mult).then_inc(omega_made, 1)
            dve.wait_ge(omega_made, 1)
            dve.sem_inc(decay_made, 1)
            ts(t(8), omega[:, :], 1.0 / TWO_PI, ROUND, ALU.mult, ALU.add)
            ts(t(8), t(8), ROUND, None, ALU.subtract, ALU.bypass)
            stt(t(9), t(8), -TWO_PI_HI, omega[:, :], ALU.mult, ALU.add)
            stt(t(9), t(8), -TWO_PI_MID, t(9), ALU.mult, ALU.add)
            stt(t(9), t(8), -TWO_PI_LO, t(9), ALU.mult, ALU.add)
            nc.vector.tensor_scalar(t(9), t(9), PI_IN, -PI_IN, ALU.min, ALU.max).then_inc(trig_in, 1)
            def angles(g, p, first):
                dve.wait_ge(phase_made, g + 1)
                off_t = off_turns[:, :].unsqueeze(1).to_broadcast([P, HG, SEG])
                off_r = off_rad[:, :].unsqueeze(1).to_broadcast([P, HG, SEG])
                ph, tu, an = phase[:, p, :, :], turns[:, p, :, :], angle[:, p, :, :]
                nc.vector.scalar_tensor_tensor(tu, ph, 1.0 / TWO_PI, off_t, ALU.mult, ALU.add).then_inc(angle_steps, 1)
                dve.wait_ge(angle_steps, 6 * g + 1)
                nc.vector.tensor_scalar(tu, tu, ROUND, ROUND, ALU.add, ALU.subtract).then_inc(angle_steps, 1)
                dve.wait_ge(angle_steps, 6 * g + 2)
                if not first:
                    dve.wait_ge(wave_made, g - 1)
                nc.vector.scalar_tensor_tensor(an, tu, -TWO_PI_HI, ph, ALU.mult, ALU.add).then_inc(angle_steps, 1)
                dve.wait_ge(angle_steps, 6 * g + 3)
                nc.vector.scalar_tensor_tensor(an, tu, -TWO_PI_MID, an, ALU.mult, ALU.add).then_inc(angle_steps, 1)
                dve.wait_ge(angle_steps, 6 * g + 4)
                nc.vector.scalar_tensor_tensor(an, tu, -TWO_PI_LO, an, ALU.mult, ALU.add).then_inc(angle_steps, 1)
                dve.wait_ge(angle_steps, 6 * g + 5)
                nc.vector.tensor_tensor(an, an, off_r, ALU.add).then_inc(angle_steps, 1)
                dve.wait_ge(angle_steps, 6 * g + 6)
                nc.vector.tensor_scalar(an, an, PI_IN, -PI_IN, ALU.min, ALU.max).then_inc(angle_made, 1)

            angles(0, 0, True)
            ts(t(12), decay[:, :], -20.0, 1.0 / 16.0, ALU.max, ALU.mult)
            ts(t(13), t(12), 1.0 / math.factorial(EXP_TERMS), None, ALU.mult, ALU.bypass)
            for n in range(EXP_TERMS - 1, 0, -1):
                stt(t(13), t(13), 1.0 / math.factorial(n), t(12), ALU.add, ALU.mult)
            for n in range(4):
                stt(t(13), t(13), 2.0, t(13), ALU.add, ALU.mult)
            dve.wait_ge(square_made, 1)
            link(nc.vector.reciprocal(t(22), t(22)))
            dve.wait_ge(half_sin, 1)
            links(vec.scalar_tensor_tensor(t(14), t(10), 2.0, t(10), ALU.mult, ALU.mult),
                  vec.scalar_tensor_tensor(t(16), t(13), 1.0, t(11), ALU.add, ALU.mult))
            cre, cim = par[:, CRE, :], par[:, CIM, :]
            links(vec.tensor_scalar(t(15), t(14), -1.0, 1.0, ALU.mult, ALU.add),
                  vec.tensor_tensor(t(18), cim, t(16), ALU.mult),
                  vec.tensor_tensor(t(19), cre, t(16), ALU.mult))
            tt(t(15), t(15), t(13), ALU.mult)
            tt(t(15), t(15), t(14), ALU.subtract)
            links(vec.tensor_tensor(t(17), cre, t(15), ALU.mult),
                  vec.tensor_tensor(t(20), cim, t(15), ALU.mult))
            links(vec.tensor_tensor(t(17), t(17), t(18), ALU.subtract),
                  vec.tensor_tensor(t(19), t(19), t(20), ALU.add))
            links(vec.tensor_tensor(t(20), t(19), a_imag, ALU.mult),
                  vec.tensor_tensor(t(21), t(17), a_abs, ALU.mult),
                  vec.tensor_tensor(t(14), t(19), a_abs, ALU.mult),
                  vec.tensor_tensor(t(15), t(17), a_imag, ALU.mult))
            links(vec.tensor_tensor(t(20), t(20), t(21), ALU.subtract),
                  vec.tensor_tensor(t(14), t(14), t(15), ALU.add))
            vec.scalar_tensor_tensor(cs_re[:, :], t(20), 2.0, t(22), ALU.mult, ALU.mult).then_inc(coef_made, 1)
            vec.scalar_tensor_tensor(cs_im[:, :], t(14), -2.0, t(22), ALU.mult, ALU.mult).then_inc(coef_made, 1)

            def kernel_rows(g, p, i, first):
                dve.wait_ge(k_made, g + 1)
                if not first:
                    dve.wait_ge(k_stored[p], 16 * i)
                nc.vector.tensor_copy(k_sb[:, p, :, :], k_ps[:, :, :]).then_inc(k_copied, 1)
                dve.wait_ge(k_copied, g + 1)
                nc.vector.tensor_tensor(k_sb[0:1, p, :, 0], k_sb[0:1, p, :, 0], skip_row[0:1, hs(g)],
                                        ALU.add).then_inc(k_added, 1)

            def outputs(g, p, first):
                if not first:
                    dve.wait_ge(post_done, g - 1)
                for h in range(HG):
                    dve.wait_ge(conv_done, g * HG + h + 1)
                    nc.vector.tensor_tensor(y_t[:, p, :, h * B:(h + 1) * B],
                                            conv_ps[:, h, 0:C * B].rearrange("p (c b) -> p c b", c=C),
                                            mask_t[:, :, :], ALU.mult).then_inc(conv_read, 1)

            def router(g, p):
                dve.wait_ge(ytr_read, 2 * g + 2)
                nc.vector.reduce_sum(logits[:, bass.ds(g, 1), :], y_tok[:, p, :, P:].rearrange("p c e -> p e c"),
                                     AX.X).then_inc(log_made, 1)

            def choose(lo, hi):
                for g in range(lo, hi):
                    nc.vector.max(top_v[:, g, :], logits[:, g, :]).then_inc(top_found, 1)
                dve.wait_ge(top_found, hi)
                for g in range(lo, hi):
                    nc.vector.max_index(top_i[:, g, :], top_v[:, g, :], logits[:, g, :]).then_inc(top_made, 1)
                dve.wait_ge(top_made, hi)
                n = hi - lo
                link(nc.vector.tensor_copy(expert[:, :, lo:hi], top_i[:, lo:hi, 0:K].rearrange("p g k -> p k g")))
                links(*[nc.vector.tensor_tensor(chosen[:, k, lo:hi, :],
                                                expert[:, k, lo:hi].unsqueeze(2).to_broadcast([P, n, E]),
                                                iota_row[:, 0:E].unsqueeze(1).to_broadcast([P, n, E]),
                                                ALU.is_equal) for k in range(K)])
                nc.vector.tensor_tensor(both[:, :, lo:hi].rearrange("p e g -> p g e"), chosen[:, 0, lo:hi, :],
                                        chosen[:, 1, lo:hi, :], ALU.add).then_inc(chosen_made, 1)
                tt(spread[:, lo:hi, :], logits[:, lo:hi, :], top_v[:, lo:hi, 0:1].to_broadcast([P, n, E]), ALU.subtract)
                nc.vector.tensor_tensor(top2[:, :, lo:hi], top_v[:, lo:hi, 0:K].rearrange("p g k -> p k g"),
                                        top_v[:, lo:hi, 0].unsqueeze(1).to_broadcast([P, K, n]),
                                        ALU.subtract).then_inc(spread_made, 1)

            dve.wait_ge(len_in, 16)
            dve.wait_ge(consts_made, 1)
            link(nc.vector.tensor_copy(len_f[:, :], len_i[:, :]))
            for c in range(C):
                last = nc.vector.tensor_scalar(mask_t[:, c, :], len_f[:, :], time_col[:, c:c + 1], None,
                                               ALU.is_gt, ALU.bypass)
            last.then_inc(mask_ready, 1)
            kernel_rows(0, 0, 0, True)
            angles(1, 1, True)
            angles(2, 0, False)
            kernel_rows(1, 1, 0, True)
            angles(3, 1, False)
            dve.wait_ge(mask_ready, 1)
            kernel_rows(2, 0, 1, False)
            outputs(0, 0, True)
            angles(4, 0, False)
            kernel_rows(3, 1, 1, False)
            outputs(1, 1, True)
            router(0, 0)
            angles(5, 1, False)
            with dve.Fori(1, (G - 4) // 2) as i:
                for p in range(2):
                    kernel_rows(2 * i + 2 + p, p, i + 1, False)
                    outputs(2 * i + p, p, False)
                    router(2 * i + p - 1, 1 - p)
                    angles(2 * i + 4 + p, p, False)
            for g in range(G - 4, G):
                if g + 2 < G:
                    kernel_rows(g + 2, g % 2, (g + 2) // 2, False)
                if g == G - 1:
                    dve.wait_ge(log_made, G - 2)
                    choose(0, G - 2)
                outputs(g, g % 2, False)
                router(g - 1, (g - 1) % 2)
            router(G - 1, (G - 1) % 2)

            dve.wait_ge(log_made, G)
            choose(G - 2, G)
            dve.wait_ge(starts_marked, 1)
            dve.wait_ge(counted, 1)
            link(nc.vector.tensor_tensor_scan(run[:, :, :].rearrange("p e g -> p (e g)"),
                                              not_first[:, :, :].rearrange("p e g -> p (e g)"),
                                              conv_ps[:, 1, 0:E * G], 0.0, ALU.mult, ALU.add))
            dve.wait_ge(spread_exp, 1)
            links(vec.tensor_scalar(tiles[:, :], run[:, :, G - 1], 1.0 / P, HALF_DOWN, ALU.mult, ALU.add),
                  vec.reduce_sum(total[:, :], spread[:, :, :], AX.X))
            links(vec.tensor_scalar(tiles[:, :], tiles[:, :], ROUND, ROUND, ALU.add, ALU.subtract),
                  vec.reciprocal(total[:, :], total[:, :]))
            links(vec.tensor_scalar(tiles[:, :], tiles[:, :], 1.0, None, ALU.max, ALU.bypass),
                  vec.tensor_tensor(weight[:, :, :], top2[:, :, :], total[:, :].unsqueeze(1).to_broadcast([P, K, G]),
                                    ALU.mult))
            links(vec.tensor_tensor_scan(ends[:, :], ones[:, 0:E], tiles[:, :], 0.0, ALU.mult, ALU.add),
                  vec.tensor_tensor(norm[:, :], weight[:, 0, :], weight[:, 1, :], ALU.add))
            vec.tensor_copy(ends_i[:, :], ends[:, :]).then_inc(ends_made, 1)
            links(vec.tensor_tensor(starts[:, :], ends[:, :], tiles[:, :], ALU.subtract),
                  vec.reciprocal(norm[:, :], norm[:, :]))
            links(vec.tensor_tensor(weight[:, :, :], weight[:, :, :], norm[:, :].unsqueeze(1).to_broadcast([P, K, G]),
                                    ALU.mult),
                  vec.tensor_tensor(dest[:, :, :], run[:, :, :], later_ps, ALU.add))
            stt(dest[:, :, :], starts[:, :].unsqueeze(2).to_broadcast([P, E, G]), float(P), dest[:, :, :],
                ALU.mult, ALU.add)
            links(*[nc.vector.tensor_tensor(chosen[:, k, :, :], chosen[:, k, :, :],
                                            dest[:, :, :].rearrange("p e g -> p g e"), ALU.mult) for k in range(K)])
            link(nc.vector.reduce_sum(slot[:, :], chosen[:, :, :, :].rearrange("p k g e -> p (k g) e"), AX.X))
            ts(slot_q[:, :], slot[:, :], 1.0 / P, -HALF_DOWN, ALU.mult, ALU.add)
            ts(slot_q[:, :], slot_q[:, :], ROUND, ROUND, ALU.add, ALU.subtract)
            stt(slot[:, :], slot_q[:, :], -float(P), slot[:, :], ALU.mult, ALU.add)
            for q, (lo, hi) in enumerate(PIECES):
                js = slice(lo, hi)
                col = [P, hi - lo, MC]
                nc.vector.tensor_tensor(slot_hot[:, js, :], slot_q[:, js].unsqueeze(2).to_broadcast(col),
                                        iota_row[:, 0:MC].unsqueeze(1).to_broadcast(col),
                                        ALU.is_equal).then_inc(hot_made, 1)
                nc.vector.tensor_tensor(slot_row[:, js, :], slot[:, js].unsqueeze(2).to_broadcast([P, hi - lo, P]),
                                        iota_row[:, :].unsqueeze(1).to_broadcast([P, hi - lo, P]),
                                        ALU.is_equal).then_inc(hot_row_made, 1)
            dve.wait_ge(table_made, 1)
            ts(shift[:, :], table_ps[:, 0:MC], 0.0, float(NONE), ALU.is_equal, ALU.mult)
            stt(named[:, :], table_ps[:, 0:MC], -1.0, shift[:, :], ALU.add, ALU.add)
            nc.vector.tensor_copy(from_row[:, :], named[:, :]).then_inc(sources_made, 1)
            dve.wait_ge(sources_made, 1)
            ts(shift[:, :], table_ps[:, 0:MC], 0.0, spare[:, 0:1], ALU.is_equal, ALU.mult)
            stt(named[:, :], table_ps[:, 0:MC], -1.0, shift[:, :], ALU.add, ALU.add)
            link(nc.vector.tensor_copy(slot_weight[:, :], table_ps[:, MC:]))
            nc.vector.tensor_copy(to_row[:, :], named[:, :]).then_inc(lists_made, 1)
            tt(passed[:, :, :], iota_row[:, 0:MC].unsqueeze(2).to_broadcast([P, MC, E]),
               ends[:, :].unsqueeze(1).to_broadcast([P, MC, E]), ALU.is_ge)
            link(nc.vector.reduce_sum(tile_e[:, :], passed[:, :, :], AX.X))
            ts(tile_e[:, :], tile_e[:, :], float(E - 1), None, ALU.min, ALU.bypass)
            ts(tile_f[:, 1, :], tile_e[:, :], 1.0, None, ALU.add, ALU.bypass)
            ts(tile_f[:, 0, :], tile_e[:, :], 1.0 / WB, -(WB - 1) / (2.0 * WB), ALU.mult, ALU.add)
            ts(tile_f[:, 0, :], tile_f[:, 0, :], ROUND, ROUND, ALU.add, ALU.subtract)
            stt(tile_f[:, 0, :], tile_f[:, 0, :], -float(WB), tile_e[:, :], ALU.mult, ALU.add)
            nc.vector.tensor_copy(tile_i[:, :, :], tile_f[:, :, :]).then_inc(experts_made, 1)

            def turn_rest(t, p, first):
                dve.wait_ge(turned, t + 1)
                if not first:
                    dve.wait_ge(gu_done, t - 1)
                nc.vector.tensor_copy(ys_t[:, p, C // 2:, :], ytr_ps[:, L // 2:].rearrange("p (c n) -> p c n", n=P)
                                      ).then_inc(yst_dve, 1)

            def hidden(t, p, first):
                dve.wait_ge(silu_made, t + 1)
                if not first:
                    dve.wait_ge(hid_turned, t - 1)
                nc.vector.tensor_tensor(hid[:, p, :], silu[:, p, :], gu_ps[:, INTER:], ALU.mult).then_inc(hid_made, 1)

            def hidden_turned(t, p, first):
                dve.wait_ge(hid_turned, t + 1)
                if not first:
                    dve.wait_ge(down_done, t - 1)
                nc.vector.tensor_copy(hid_t[:, p, :], hid_ps).then_inc(hid_read, 1)

            def weight_of(t, p, first):
                if not first:
                    dve.wait_ge(od_act, t - 1)
                    dve.wait_ge(od_dve, t - 1)
                nc.vector.tensor_copy(weight_now[:, p:p + 1], slot_weight[:, bass.ds(t, 1)]).then_inc(weight_copied, 1)

            def weigh_rest(t, p, i, first):
                dve.wait_ge(down_done, t + 1)
                dve.wait_ge(weight_copied, t + 1)
                if not first:
                    dve.wait_ge(scattered[p], 16 * i)
                nc.vector.tensor_scalar(od[:, p, L // 2:], down_ps[:, 1, :], weight_now[:, p:p + 1], None,
                                        ALU.mult, ALU.bypass).then_inc(od_dve, 1)

            turn_rest(0, 0, True)
            weight_of(0, 0, True)
            hidden(0, 0, True)
            turn_rest(1, 1, True)
            hidden_turned(0, 0, True)
            weight_of(1, 1, True)
            hidden(1, 1, True)
            turn_rest(2, 0, False)
            weigh_rest(0, 0, 0, True)
            hidden_turned(1, 1, True)
            weight_of(2, 0, False)
            hidden(2, 0, False)
            turn_rest(3, 1, False)
            weigh_rest(1, 1, 0, True)
            hidden_turned(2, 0, False)

            def pair(i):
                for p in (1, 0):
                    weight_of(2 * i + 2 - p, p, False)
                    hidden(2 * i + 2 - p, p, False)
                    turn_rest(2 * i + 3 - p, 1 - p, False)
                    weigh_rest(2 * i + 1 - p, 1 - p, i, False)
                    hidden_turned(2 * i + 2 - p, p, False)

            used = tiles_in_use(dve)
            pairs(dve, used, pair)
            with dve.If(used >= MT - 2):
                for t in range(MT - 2, MT):
                    weight_of(t, t % 2, False)
                    hidden(t, t % 2, False)
                    if t + 1 < MT:
                        turn_rest(t + 1, (t + 1) % 2, False)
                    weigh_rest(t - 1, (t - 1) % 2, (t - 1) // 2, False)
                    hidden_turned(t, t % 2, False)
                weigh_rest(MT - 1, (MT - 1) % 2, (MT - 1) // 2, False)

        @block.tensor
        def _(pe):
            def products(g, p, first):
                pe.wait_ge(factors_made, g + 1)
                if not first:
                    pe.wait_ge(k_copied, g)
                for h in range(HG):
                    last = nc.tensor.matmul(k_ps[:, h, :], am[:, p, h, :], bm[:, p, h, :], start=True, stop=True)
                last.then_inc(k_made, 1)

            def convolve_channel(g, h, p, first):
                if not first:
                    pe.wait_ge(conv_read, g * HG + h - HG + 1)
                for d in range(C):
                    last = nc.tensor.matmul(conv_ps[:, h, d * B:C * B], toep[:, p, h, d * P:(d + 1) * P],
                                            u_t[:, p, h, 0:(C - d) * B], start=(d == 0), stop=(d == C - 1))
                last.then_inc(conv_done, 1)

            def convolve_first(g, between):
                pe.wait_ge(u_in[g], 16)
                for h in range(HG):
                    pe.wait_ge(toep_first[g][h], 16)
                    convolve_channel(g, h, g, g == 0)
                    if h == 0:
                        between()

            def convolve(g, p, i, between=None):
                pe.wait_ge(u_in[p], 16 * (i + 1))
                pe.wait_ge(toep_in[p], 16 * i)
                for h in range(HG):
                    convolve_channel(g, h, p, False)
                    if h == 0 and between:
                        between()

            def stay_awake(n, bank):
                for _ in range(n):
                    nc.tensor.matmul(bank, ones[:, :], ones[:, :], start=True, stop=True)

            def post(g, p, first):
                pe.wait_ge(conv_read, g * HG + HG)
                if not first:
                    pe.wait_ge(ytr_read, 2 * g)
                for c in range(C):
                    last = nc.tensor.matmul(turn_ps[:, c // IGS, c % IGS * IG:(c % IGS + 1) * IG], y_t[:, p, c, :],
                                            ident_gate[:, c, :], start=True, stop=True)
                last.then_inc(post_done, 1)

            pe.wait_ge(gate_in, 16)
            pe.wait_ge(consts_made, 1)
            pe.wait_ge(coef_made, 2)
            stay_awake(4, turn_ps[:, 2, 0:P])
            products(0, 0, True)
            stay_awake(21, turn_ps[:, 2, 0:P])
            convolve_first(0, lambda: products(1, 1, False))
            for g in range(2, 4):
                products(g, g % 2, False)
            convolve_first(1, lambda: None)
            pe.wait_ge(ident_copied, 1)
            post(0, 0, True)
            products(4, 0, False)
            with pe.Fori(1, (G - 4) // 2) as i:
                for p in range(2):
                    convolve(2 * i + p, p, i)
                    post(2 * i + p - 1, 1 - p, False)
                    products(2 * i + 3 + p, 1 - p, False)
            for g in range(G - 4, G):
                if g + 1 == G:
                    convolve(g, g % 2, g // 2, lambda: post(g - 1, (g - 1) % 2, False))
                    continue
                convolve(g, g % 2, g // 2)
                post(g - 1, (g - 1) % 2, False)
                if g + 3 < G:
                    products(g + 3, (g + 3) % 2, False)
            post(G - 1, (G - 1) % 2, False)

            stay_awake(8, k_bank[:, :, :])
            pe.wait_ge(chosen_made, 2)
            nc.tensor.matmul(later_ps, not_before[:, :], both[:, :, :], start=True, stop=True)
            nc.tensor.matmul(count_ps, ones[:, :], both[:, :, :], start=True, stop=True).then_inc(counted, 1)
            stay_awake(30, k_bank[:, :, :])
            for q, (lo, hi) in enumerate(PIECES):
                pe.wait_ge(hot_row_made, q + 1)
                pe.wait_ge(hot_weight_made, q + 1)
                pe.wait_ge(hot_token_made, q + 1)
                for j in range(lo, hi):
                    last = nc.tensor.matmul(table_ps, slot_row[:, j, :], slot_tile[:, j, :],
                                            start=(j == 0), stop=(j == K * G - 1))
            last.then_inc(table_made, 1)
            stay_awake(20, k_bank[:, :, :])

            def gate_up(t, p):
                buf = pe.value_load(tile_i[0:1, 0, bass.ds(t, 1)], min_val=0, max_val=WB - 1)
                need = pe.value_load(tile_i[0:1, 1, bass.ds(t, 1)], min_val=1, max_val=E)
                pe.wait_ge(weights_ready, need)
                pe.wait_ge(yst_act, t + 1)
                pe.wait_ge(yst_dve, t + 1)
                for c in range(C):
                    last = nc.tensor.matmul(gu_ps, ys_t[:, p, c, :], w_gu[:, bass.ds(buf * (C * GU) + c * GU, GU)],
                                            start=(c == 0), stop=(c == C - 1))
                last.then_inc(gu_done, 1)

            def turn(t, p, i):
                pe.wait_ge(gathered[p], 16 * (i + 1))
                for c in range(C):
                    last = nc.tensor.transpose(ytr_ps[:, c * P:(c + 1) * P], ys[:, p, c * P:(c + 1) * P], ident[:, :])
                last.then_inc(turned, 1)

            def down(t, p, first):
                buf = pe.value_load(tile_i[0:1, 0, bass.ds(t, 1)], min_val=0, max_val=WB - 1)
                pe.wait_ge(hid_read, t + 1)
                if not first:
                    pe.wait_ge(od_act, t)
                    pe.wait_ge(od_dve, t)
                for n in range(2):
                    last = nc.tensor.matmul(down_ps[:, n, :], hid_t[:, p, :],
                                            w_d[:, bass.ds(buf * L + n * (L // 2), L // 2)], start=True, stop=True)
                last.then_inc(down_done, 1)

            def turn_hidden(t, p):
                pe.wait_ge(hid_made, t + 1)
                nc.tensor.transpose(hid_ps, hid[:, p, :], ident[:, :]).then_inc(hid_turned, 1)

            turn(0, 0, 0)
            pe.wait_ge(experts_made, 1)
            gate_up(0, 0)
            turn(1, 1, 0)
            turn_hidden(0, 0)
            gate_up(1, 1)
            turn(2, 0, 1)
            down(0, 0, True)
            turn_hidden(1, 1)
            gate_up(2, 0)
            turn(3, 1, 1)
            down(1, 1, False)
            turn_hidden(2, 0)

            def pair(i):
                for p in (1, 0):
                    gate_up(2 * i + 2 - p, p)
                    turn(2 * i + 3 - p, 1 - p, i + 1)
                    down(2 * i + 1 - p, 1 - p, False)
                    turn_hidden(2 * i + 2 - p, p)

            used = tiles_in_use(pe)
            pairs(pe, used, pair)
            with pe.If(used >= MT - 2):
                for t in range(MT - 2, MT):
                    gate_up(t, t % 2)
                    if t + 1 < MT:
                        turn(t + 1, (t + 1) % 2, (t + 1) // 2)
                    down(t - 1, (t - 1) % 2, False)
                    turn_hidden(t, t % 2)
                down(MT - 1, (MT - 1) % 2, False)


def kernel(x, itok_B_8_3872, L0_cond_log_dt, L0_cond_C, L0_cond_log_A_real, L0_cond_A_imag, L0_cond_D,
           L0_ffn_gate_w, L0_ffn_u, L0_ffn_g, L0_ffn_d):
    import numpy as np
    import concourse.bacc as bacc
    from concourse.bass_utils import run_bass_kernel_spmd

    x = np.asarray(x)
    c = np.asarray(L0_cond_C)
    gu = np.stack([np.asarray(L0_ffn_g), np.asarray(L0_ffn_u)]).reshape(2, E, INTER, C, P)
    arrays = {
        "x_time": x.reshape(B, H, C, P)[:, :, :, ::-1].transpose(3, 1, 2, 0).reshape(P, H, C * B),
        "x_rows": x.transpose(1, 0, 2).reshape(TOK, L),
        "lengths": np.asarray(itok_B_8_3872),
        "params": np.tile(np.stack([np.broadcast_to(np.asarray(L0_cond_log_dt), (N, H)),
                                    np.asarray(L0_cond_log_A_real).T, np.asarray(L0_cond_A_imag).T,
                                    c[:, :, 0].T, c[:, :, 1].T], axis=1), (2, 1, 1)),
        "skip": np.asarray(L0_cond_D).reshape(1, H),
        "gate_t": np.asarray(L0_ffn_gate_w).reshape(E, C, P).transpose(2, 1, 0),
        "gu_t": gu.transpose(1, 4, 3, 0, 2).reshape(E, P, C * 2 * INTER),
        "d_t": np.asarray(L0_ffn_d).reshape(L, E, INTER).transpose(1, 2, 0),
    }
    arrays = {name: np.ascontiguousarray(a) for name, a in arrays.items()}
    nc = bacc.Bacc("TRN2", target_bir_lowering=False, num_devices=1)
    ins = [nc.dram_tensor(name, a.shape, mybir.dt.from_np(a.dtype), kind="ExternalInput").ap()
           for name, a in arrays.items()]
    out = nc.dram_tensor("out", (TOK + P, L), mybir.dt.float32, kind="ExternalOutput").ap()
    build(nc, *ins, out)
    got = run_bass_kernel_spmd(nc, [arrays], core_ids=[0]).results[0]["out"]
    return np.ascontiguousarray(got[:TOK].reshape(H, B, L).transpose(1, 0, 2))
```
